# Optimizing a Trainium2 kernel written in Bass

```python
import numpy as np
import jax
import jax.numpy as jnp

def _softmax(x, axis=-1):
    return jax.nn.softmax(x, axis=axis)

def _gelu(x):
    return jax.nn.gelu(x, approximate=True)

def _silu(x):
    return jax.nn.silu(x)

def _sigmoid(x):
    return jax.nn.sigmoid(x)

def _layernorm(x, axis=-1, eps=1e-05):
    m = jnp.mean(x, axis=axis, keepdims=True)
    v = jnp.var(x, axis=axis, keepdims=True)
    return (x - m) / jnp.sqrt(v + eps)

def _scatter_add(tgt, idx, src, axis=0):
    return tgt.at[idx].add(src)

def _segment_sum(src, seg, n):
    return jax.ops.segment_sum(src, seg, n)
kernel_name = 'mk_xattn_seq_d1_seqx_r2_0a49e6'

def setup_inputs(seed: int=0):
    np.random.seed(seed)
    _w = jnp.asarray

    def _rec_inputs():
        import jax
        import jax.numpy as jnp
        _rk = jax.random.key(seed)
        x = -0.0005207 + 1.001 * jax.random.normal(jax.random.fold_in(_rk, 1), (8, 1024, 512), jnp.float32)
        _lenS = 1024 - jax.random.randint(jax.random.fold_in(_rk, 7), (8,), 0, max(1, 1024 // 4) + 1, jnp.int32)
        _lenS2 = 64 - jax.random.randint(jax.random.fold_in(_rk, 8), (8,), 0, max(1, 64 // 4) + 1, jnp.int32)
        _ctx_1024P = jax.random.normal(jax.random.fold_in(_rk, 11), (8, 16, 512), jnp.float32)
        _ctx_1024c = jax.random.dirichlet(jax.random.fold_in(_rk, 511), 0.3 * jnp.ones((16,), jnp.float32), (8, 64))
        _ctx_1024t = jnp.einsum('bsk,bkd->bsd', _ctx_1024c, _ctx_1024P)
        _ctx_1024t = _ctx_1024t * jax.lax.rsqrt(jnp.mean(jnp.square(_ctx_1024t)) + 1e-12) * 0.953939
        ctx_1024 = 4.13588e-05 + 0.999923 * (_ctx_1024t + 0.3 * jax.random.normal(jax.random.fold_in(_rk, 611), (8, 64, 512), jnp.float32))
        return (x, ctx_1024)
    x, ctx_1024 = _rec_inputs()

    def _L0_xattn_setup():
        import jax, jax.numpy as jnp
        import numpy as np
        B, S, R, D, H, FF = (2, 512, 4, 512, 16, 2048)
        HD = D // H
        NEG_INF = jnp.float32(-jnp.inf)

        def _layer_norm(x, g, b, eps=1e-05):
            m = jnp.mean(x, axis=-1, keepdims=True)
            v = jnp.mean((x - m) ** 2, axis=-1, keepdims=True)
            return (x - m) * jax.lax.rsqrt(v + eps) * g + b

        def _forward(query, context, wq, wk, wv, bq, bk, bv, wo, bo, ln1_g, ln1_b, ln2_g, ln2_b, w1, b1, w2, b2):
            Bq, Sq, Dm = query.shape
            Sc = context.shape[1]
            hd = Dm // H
            q = _layer_norm(query, ln1_g, ln1_b)
            qh = (q @ wq + bq).reshape(Bq, Sq, H, hd)
            kh = (context @ wk + bk).reshape(Bq, Sc, H, hd)
            vh = (context @ wv + bv).reshape(Bq, Sc, H, hd)
            scale = 1.0 / jnp.sqrt(jnp.float32(hd))
            scores = jnp.einsum('bqhd,bkhd->bhqk', qh, kh) * scale
            pos_in_block = jnp.arange(Sc) % Sq
            allowed = pos_in_block[None, :] <= jnp.arange(Sq)[:, None]
            scores = jnp.where(allowed[None, None, :, :], scores, NEG_INF)
            probs = jax.nn.softmax(scores, axis=-1)
            o = jnp.einsum('bhqk,bkhd->bqhd', probs, vh).reshape(Bq, Sq, Dm)
            attn_out = o @ wo + bo
            x = query + attn_out
            h = _layer_norm(x, ln2_g, ln2_b)
            ff = jax.nn.gelu(h @ w1 + b1, approximate=False) @ w2 + b2
            return x + ff
        key = jax.random.key(seed)
        ks = jax.random.split(key, 10)
        sc = 0.02
        return {'query': jax.random.normal(ks[0], (B, S, D), dtype=jnp.float32), 'context': jax.random.normal(ks[1], (B, S * R, D), dtype=jnp.float32), 'wq': jax.random.normal(ks[2], (D, D), dtype=jnp.float32) * sc, 'wk': jax.random.normal(ks[3], (D, D), dtype=jnp.float32) * sc, 'wv': jax.random.normal(ks[4], (D, D), dtype=jnp.float32) * sc, 'bq': jnp.zeros((D,), jnp.float32), 'bk': jnp.zeros((D,), jnp.float32), 'bv': jnp.zeros((D,), jnp.float32), 'wo': jax.random.normal(ks[5], (D, D), dtype=jnp.float32) * sc, 'bo': jnp.zeros((D,), jnp.float32), 'ln1_g': jnp.ones((D,), jnp.float32), 'ln1_b': jnp.zeros((D,), jnp.float32), 'ln2_g': jnp.ones((D,), jnp.float32), 'ln2_b': jnp.zeros((D,), jnp.float32), 'w1': jax.random.normal(ks[6], (D, FF), dtype=jnp.float32) * sc, 'b1': jnp.zeros((FF,), jnp.float32), 'w2': jax.random.normal(ks[7], (FF, D), dtype=jnp.float32) * sc, 'b2': jnp.zeros((D,), jnp.float32)}
    _L0_xattn_all = _L0_xattn_setup()
    _L0_xattn_in = {k: v for k, v in _L0_xattn_all.items() if k in ('wq', 'wk', 'wv', 'bq', 'bk', 'bv', 'wo', 'bo', 'ln1_g', 'ln1_b', 'ln2_g', 'ln2_b', 'w1', 'b1', 'w2', 'b2')}
    del _L0_xattn_all
    return {'x': x, 'ctx_1024': ctx_1024, 'L0_xattn_wq': _L0_xattn_in['wq'], 'L0_xattn_wk': _L0_xattn_in['wk'], 'L0_xattn_wv': _L0_xattn_in['wv'], 'L0_xattn_bq': _L0_xattn_in['bq'], 'L0_xattn_bk': _L0_xattn_in['bk'], 'L0_xattn_bv': _L0_xattn_in['bv'], 'L0_xattn_wo': _L0_xattn_in['wo'], 'L0_xattn_bo': _L0_xattn_in['bo'], 'L0_xattn_ln1_g': _L0_xattn_in['ln1_g'], 'L0_xattn_ln1_b': _L0_xattn_in['ln1_b'], 'L0_xattn_ln2_g': _L0_xattn_in['ln2_g'], 'L0_xattn_ln2_b': _L0_xattn_in['ln2_b'], 'L0_xattn_w1': _L0_xattn_in['w1'], 'L0_xattn_b1': _L0_xattn_in['b1'], 'L0_xattn_w2': _L0_xattn_in['w2'], 'L0_xattn_b2': _L0_xattn_in['b2']}

def reference(x, ctx_1024, L0_xattn_wq, L0_xattn_wk, L0_xattn_wv, L0_xattn_bq, L0_xattn_bk, L0_xattn_bv, L0_xattn_wo, L0_xattn_bo, L0_xattn_ln1_g, L0_xattn_ln1_b, L0_xattn_ln2_g, L0_xattn_ln2_b, L0_xattn_w1, L0_xattn_b1, L0_xattn_w2, L0_xattn_b2):
    import jax
    import jax.numpy as jnp

    def _L0_xattn_ref(query, context, wq, wk, wv, bq, bk, bv, wo, bo, ln1_g, ln1_b, ln2_g, ln2_b, w1, b1, w2, b2):
        import jax, jax.numpy as jnp
        import numpy as np
        B, S, R, D, H, FF = (2, 512, 4, 512, 16, 2048)
        HD = D // H
        NEG_INF = jnp.float32(-jnp.inf)

        def _layer_norm(x, g, b, eps=1e-05):
            m = jnp.mean(x, axis=-1, keepdims=True)
            v = jnp.mean((x - m) ** 2, axis=-1, keepdims=True)
            return (x - m) * jax.lax.rsqrt(v + eps) * g + b

        def _forward(query, context, wq, wk, wv, bq, bk, bv, wo, bo, ln1_g, ln1_b, ln2_g, ln2_b, w1, b1, w2, b2):
            Bq, Sq, Dm = query.shape
            Sc = context.shape[1]
            hd = Dm // H
            q = _layer_norm(query, ln1_g, ln1_b)
            qh = (q @ wq + bq).reshape(Bq, Sq, H, hd)
            kh = (context @ wk + bk).reshape(Bq, Sc, H, hd)
            vh = (context @ wv + bv).reshape(Bq, Sc, H, hd)
            scale = 1.0 / jnp.sqrt(jnp.float32(hd))
            scores = jnp.einsum('bqhd,bkhd->bhqk', qh, kh) * scale
            pos_in_block = jnp.arange(Sc) % Sq
            allowed = pos_in_block[None, :] <= jnp.arange(Sq)[:, None]
            scores = jnp.where(allowed[None, None, :, :], scores, NEG_INF)
            probs = jax.nn.softmax(scores, axis=-1)
            o = jnp.einsum('bhqk,bkhd->bqhd', probs, vh).reshape(Bq, Sq, Dm)
            attn_out = o @ wo + bo
            x = query + attn_out
            h = _layer_norm(x, ln2_g, ln2_b)
            ff = jax.nn.gelu(h @ w1 + b1, approximate=False) @ w2 + b2
            return x + ff
        return _forward(query, context, wq, wk, wv, bq, bk, bv, wo, bo, ln1_g, ln1_b, ln2_g, ln2_b, w1, b1, w2, b2)
    x = _L0_xattn_ref(x, ctx_1024, L0_xattn_wq, L0_xattn_wk, L0_xattn_wv, L0_xattn_bq, L0_xattn_bk, L0_xattn_bv, L0_xattn_wo, L0_xattn_bo, L0_xattn_ln1_g, L0_xattn_ln1_b, L0_xattn_ln2_g, L0_xattn_ln2_b, L0_xattn_w1, L0_xattn_b1, L0_xattn_w2, L0_xattn_b2)
    return x

_drawn_inputs = setup_inputs


def setup_inputs(seed=0):
    import zlib

    import numpy as np

    out = dict(_drawn_inputs(seed))
    spreads = {'L0_xattn_bq': (0.0, 0.8),
     'L0_xattn_bk': (0.0, 0.8),
     'L0_xattn_bv': (0.0, 0.1),
     'L0_xattn_bo': (0.0, 0.1),
     'L0_xattn_ln1_g': (1.0, 0.6),
     'L0_xattn_ln1_b': (0.0, 0.8),
     'L0_xattn_ln2_g': (1.0, 0.2),
     'L0_xattn_ln2_b': (0.0, 0.342),
     'L0_xattn_b1': (0.0, 0.1),
     'L0_xattn_b2': (0.0, 0.1)}
    factors = {'L0_xattn_wq': 6.651, 'L0_xattn_wk': 6.537}
    for name, (base, spread) in spreads.items():
        noise = np.random.default_rng([zlib.crc32(name.encode()), seed]).standard_normal(out[name].shape)
        drawn = base * np.exp(spread * noise) if base else spread * noise
        out[name] = jnp.asarray(drawn.astype(out[name].dtype))
    for name, factor in factors.items():
        out[name] = (out[name] * factor).astype(out[name].dtype)
    return out
```

```python
from contextlib import ExitStack

import numpy as np

import concourse.bass as bass
from concourse import mybir

F32 = mybir.dt.float32
F16 = mybir.dt.float16
BF16 = mybir.dt.bfloat16
I32 = mybir.dt.int32
ALU = mybir.AluOpType
ACT = mybir.ActivationFunctionType
AX_X = mybir.AxisListType.X
AX_XY = mybir.AxisListType.XY

P = 128
D = 512
KT = D // P
HEADS = 16
HD = D // HEADS
GH = P // HD
BATCH = 8
SQ = 1024
SC = 64
NCTX = BATCH * SC
FF = 2048
NJ = FF // P
CHUNK = 512
TT = CHUNK // P
HALF = CHUNK // 2
NCHUNK = BATCH * SQ // CHUNK
NPAIR = HEADS // 2
EPS = 1e-5
MASKED = -(2.0 ** 120)

LN_SCALE = 2.0 ** 10
PROB_SCALE = 2.0 ** 14
LN_BOUND = D * 22.7

LAG = 2
GROUPS = NJ + LAG
PLAN = {
    2: [("T", 0)], 3: [("T", 1)], 4: [("T", 2)], 5: [("T", 3)],
    6: [("Q", 0)], 7: [("Q", 1)], 8: [("Q", 2)], 9: [("Q", 3)],
    10: [("S", 0)], 12: [("S", 1)], 13: [("S", 2)], 15: [("S", 3)],
    16: [("E", 0)],
    19: [("Z", 0)], 20: [("Z", 1)], 21: [("V", 0), ("V", 1)],
    22: [("Z", 2)], 23: [("Z", 3)], 24: [("V", 2), ("V", 3)],
    25: [("O", 0)], 26: [("O", 1)], 27: [("O", 2)], 28: [("O", 3)], 29: [("L", 0)],
    30: [("H", 0)], 31: [("H", 1)], 32: [("H", 2)], 33: [("H", 3)],
}


def wait(eng, sem, value):
    if isinstance(value, int) and value <= 0:
        return
    eng.wait_ge(sem, value)


def cross_attention_block(nc, x, context, wq, wk, wv, bq, bk, bv, wo, bo,
                          ln1_g, ln1_b, ln2_g, ln2_b, w1, b1, w2, b2, out):
    x_tiles = x.rearrange("b (n p) d -> (b n) p d", p=P)
    out_tiles = out.rearrange("b (n p) d -> (b n) p d", p=P)
    ctx_rows = context.rearrange("b s d -> (b s) d").rearrange("(n p) d -> p n d", p=P)

    with ExitStack() as ctx:
        def sb(name, shape, dt):
            return ctx.enter_context(nc.sbuf_tensor(name, shape, dt))

        def sem(name):
            return ctx.enter_context(nc.semaphore(name))

        wq_hi, wq_lo = (sb(n, [P, KT, D], F16) for n in ("wq_hi", "wq_lo"))
        wo_hi, wo_lo = (sb(n, [P, KT, D], F16) for n in ("wo_hi", "wo_lo"))
        w1_all = sb("w1_all", [P, 2 * KT * FF], F16)
        w1_hi = w1_all[:, 0:KT * FF].rearrange("p (k n) -> p k n", k=KT)
        w1_lo = w1_all[:, KT * FF:2 * KT * FF].rearrange("p (k n) -> p k n", k=KT)
        w2_all = sb("w2_all", [P, 2 * NJ * D], F16)
        w2_hi = w2_all[:, 0:NJ * D].rearrange("p (k n) -> p k n", k=NJ)
        w2_lo = w2_all[:, NJ * D:2 * NJ * D].rearrange("p (k n) -> p k n", k=NJ)
        PIECE = KT * D
        early = [w1_all[:, n * PIECE:(n + 1) * PIECE].rearrange("p (k n) -> p k n", k=KT) for n in range(6)]
        wk_hi, wk_lo, wv_hi, wv_lo, ctxT_hi, ctxT_lo = early
        w2_raw_view = w2_all[:, :].bitcast(F32)
        wk_raw, wv_raw, ctx_raw = (
            w2_raw_view[:, n * PIECE:(n + 1) * PIECE].rearrange("p (k n) -> p k n", k=KT) for n in range(3))
        bv_row = w2_raw_view[:, 3 * PIECE:3 * PIECE + D]
        kv_full = [w2_raw_view[:, 3 * PIECE + (1 + n) * D:3 * PIECE + (2 + n) * D] for n in range(2)]

        arena = sb("arena", [P, 10 * PIECE], F32)

        def raw(n):
            return arena[:, n * PIECE:(n + 1) * PIECE].rearrange("p (k n) -> p k n", k=KT)

        wq_raw, wo_raw = raw(0), raw(1)
        w1_raw = [raw(2 + n) for n in range(FF // D)]
        w2_raw = [raw(6 + n) for n in range(NJ // KT)]
        used = [0]

        def carve(words):
            used[0] += words
            assert used[0] <= 10 * PIECE
            return arena[:, used[0] - words:used[0]]

        x1 = [carve(TT * D).rearrange("p (t n) -> p t n", t=TT) for _ in range(2)]
        probs = [carve(HEADS * SC) for _ in range(TT)]
        pT = carve(NPAIR * HALF).bitcast(F16).rearrange("p (a g n) -> p a g n", a=2, g=NPAIR)
        pT_hi, pT_lo = pT[:, 0], pT[:, 1]
        hT = [carve(KT * CHUNK).bitcast(F16).rearrange("p (a k n) -> p a k n", a=2, k=KT) for _ in range(2)]
        gelu_full = [carve(CHUNK) for _ in range(2)]
        NG = 4
        g_pair = [carve(CHUNK).bitcast(F16).rearrange("p (a n) -> p a n", a=2) for _ in range(NG)]
        kblk = carve(KT * GH * SC).bitcast(F16).rearrange("p (a g h k) -> p a g h k", a=2, g=KT, h=GH)
        vblk = carve(NPAIR * P).bitcast(F16).rearrange("p (a m e n) -> p a m e n", a=2, m=KT, e=2)
        q_full = [carve(CHUNK) for _ in range(2)]

        x_sb = sb("x_sb", [P, TT, D], F32)
        xhat = sb("xhat", [P, 2, D], F32)
        act_T = sb("act_T", [P, 2, KT, CHUNK], F16)
        aT_hi, aT_lo = act_T[:, 0], act_T[:, 1]
        qT = sb("qT", [P, 2, KT, CHUNK], F16)
        qT_hi, qT_lo = qT[:, 0], qT[:, 1]
        kT_sb = sb("kT_sb", [P, 2, KT, NCTX], F16)
        v_sb = sb("v_sb", [P, 2, BATCH, D], F16)
        bo_row = sb("bo_row", [P, D], F32)
        b2_row = sb("b2_row", [P, D], F32)
        ident = sb("ident", [P, P], F32)
        ident_bf = sb("ident_bf", [P, P], BF16)
        causal = sb("causal", [P, GH, SC], BF16)
        mask_k = sb("mask_k", [P, GH], F16)
        mask_v = sb("mask_v", [P, 2, P], F16)
        NV = 6 * KT + NJ
        vec_rows = sb("vec_rows", [NV, P], F32)
        cols = sb("cols", [P, NV], F32)
        BQ, BK, G1, B1LN, G2, B2LN, B1F = (KT * n for n in range(7))
        bqp = sb("bqp", [P, KT], F32)
        bkp = sb("bkp", [P, KT], F32)
        b1p = sb("b1p", [P, NJ], F32)
        gs1 = sb("gs1", [P, KT], F32)
        gs2 = sb("gs2", [P, KT], F32)
        MQ, MK, MV, MO, MC, MG1, MG2, MBQ, MBK, MBV, MB1, MW1, MW2 = range(13)
        NM = 11 + 2 * (NJ // KT)
        maxima = sb("maxima", [P, NM], F32)
        gmax = sb("gmax", [P, NM], F32)
        (LQ, LK, LV, LO, L1, L2, LC, LBQ, LBK, LBV, LBG) = range(11)
        bound = sb("bound", [P, 11], F32)
        pw = sb("pw", [P, 11], F32)
        rp = sb("rp", [P, 11], F32)
        ws = sb("ws", [P, 8], F32)
        (CQ, CK, CV, CE, CO, C1, SG, C2, AQ, AK, AV_, AO, A1, A2, AC, SQ_, SK_, SV_) = range(18)
        sc = sb("sc", [P, 18], F32)
        minus_half = sb("minus_half", [P, 1], F32)
        stats = sb("stats", [P, 2 * TT, 6], F32)
        mv = sb("mv", [P, 2 * TT, 2], F32)
        ve = sb("ve", [P, 2 * TT], F32)
        rstd = sb("rstd", [P, 2 * TT], F32)
        smax = sb("smax", [P, TT, HEADS], F32)
        ssum = sb("ssum", [P, TT, HEADS], F32)
        rsum = sb("rsum", [P, TT, HEADS], F32)

        def col(n):
            return sc[:, n:n + 1]

        ff2_ps = ctx.enter_context(nc.psum_tensor("ff2_ps", [P, TT, D], F32))
        ff1_ps = ctx.enter_context(nc.psum_tensor("ff1_ps", [P, 2, CHUNK], F32))
        at_ps = ctx.enter_context(nc.psum_tensor("at_ps", [P, 2, CHUNK], F32))
        scores = at_ps[:, :, :].rearrange("p a (h k) -> p (a h) k", k=SC)

        NW = 12
        w_loaded = [sem(f"w_loaded{n}") for n in range(NW)]
        W_K, W_V, W_Q, W_O, W_1, W_2 = 0, 1, 2, 3, 4, 8
        ctx_loaded = sem("ctx_loaded")
        vecs_loaded = sem("vecs_loaded")
        rows_loaded = sem("rows_loaded")
        const_set = sem("const_set")
        const_dve = sem("const_dve")
        cols_ps = sem("cols_ps")
        cols_set = sem("cols_set")
        ctxT_ps = sem("ctxT_ps")
        biases_ps = sem("biases_ps")
        max_ready = sem("max_ready")
        gmax_ready = sem("gmax_ready")
        scales_ready = sem("scales_ready")
        chain = sem("chain")
        pool_chain = sem("pool_chain")
        conv_hi = sem("conv_hi")
        conv_lo = sem("conv_lo")
        kv_ps = sem("kv_ps")
        k_full_set = sem("k_full_set")
        kv_out = sem("kv_out")
        x_loaded = [sem(f"x_loaded{t}") for t in range(TT)]
        out_stored = [sem(f"out_stored{t}") for t in range(TT)]
        ln_mv, ln_ve, ln_rstd, ln_out = (sem(n) for n in ("ln_mv", "ln_ve", "ln_rstd", "ln_out"))
        xb_set = sem("xb_set")
        x1b_set = sem("x1b_set")
        blk_set = sem("blk_set")
        (t_ps, q_ps, s_ps, z_ps, v_ps, o_ps, h_ps, ff1_done, ff2_done) = (sem(n) for n in (
            "t_ps", "q_ps", "s_ps", "z_ps", "v_ps", "o_ps", "h_ps", "ff1_done", "ff2_done"))
        t_hi, t_lo, q_out, q_hi, q_lo, s_max, s_sub, e_set, s_sum, s_rec, p_norm = (sem(n) for n in (
            "t_hi", "t_lo", "q_out", "q_hi", "q_lo", "s_max", "s_sub", "e_set", "s_sum", "s_rec", "p_norm"))
        z_hi, z_lo, v_hi, v_lo, x1_set, h_hi, h_lo, g_full, g_hi, g_lo, out_set = (sem(n) for n in (
            "z_hi", "z_lo", "v_hi", "v_lo", "x1_set", "h_hi", "h_lo", "g_full", "g_hi", "g_lo", "out_set"))

        ctxT_banks = [ff2_ps[:, k, :] for k in range(KT)]
        conversions = [(ctxT_banks[k], col(AC), ctxT_hi[:, k], ctxT_lo[:, k]) for k in range(KT)]
        conversions += [(wk_raw, col(AK), wk_hi, wk_lo), (wv_raw, col(AV_), wv_hi, wv_lo)]
        KV_CONV = len(conversions)
        conversions += [(wq_raw[:, k], gs1[:, k:k + 1], wq_hi[:, k], wq_lo[:, k]) for k in range(KT)]
        conversions += [(wo_raw, col(AO), wo_hi[:, :, :], wo_lo[:, :, :])]
        OVERLAID = len(conversions)
        for n in range(FF // D):
            conversions += [(w1_raw[n][:, k], gs2[:, k:k + 1], w1_hi[:, k, n * D:(n + 1) * D],
                             w1_lo[:, k, n * D:(n + 1) * D]) for k in range(KT)]
        for n in range(NJ // KT):
            conversions += [(w2_raw[n], col(A2), w2_hi[:, n * KT:(n + 1) * KT], w2_lo[:, n * KT:(n + 1) * KT])]
        NCONV = len(conversions)

        def slots(eng, slot, loads=False):
            slot(0, 0, True, False, 0)
            slot(1, 1, True, True, None)
            with eng.Fori(0, BATCH - 1 - loads) as i:
                slot(2 * i + 2, 0, True, True, i + 1)
                slot(2 * i + 3, 1, True, True, None)
            if loads:
                slot(NCHUNK - 2, 0, True, True, BATCH - 1)
                slot(NCHUNK - 1, 1, True, True, None)
            slot(NCHUNK, 0, False, True, None)

        block = ctx.enter_context(nc.Block())

        @block.sync
        def _(sp):
            row = 0
            for v in (bq, bk, ln1_g, ln1_b, ln2_g, ln2_b, b1):
                n = v.shape[0] // P
                sp.dma_start(vec_rows[row:row + n, :], v.rearrange("(k p) -> k p", p=P)).then_inc(vecs_loaded, 16)
                row += n
            sp.dma_start(ctx_raw, ctx_rows).then_inc(ctx_loaded, 16)
            sp.dma_start(wk_raw, wk.rearrange("(k p) n -> p k n", p=P)).then_inc(w_loaded[W_K], 16)
            sp.dma_start(wv_raw, wv.rearrange("(k p) n -> p k n", p=P)).then_inc(w_loaded[W_V], 16)
            sp.dma_start(wq_raw, wq.rearrange("(k p) n -> p k n", p=P)).then_inc(w_loaded[W_Q], 16)
            for v, dst in ((bv, bv_row), (bo, bo_row[:, :]), (b2, b2_row[:, :])):
                sp.dma_start(dst, v.rearrange("(a n) -> a n", a=1).to_broadcast([P, D])).then_inc(rows_loaded, 16)
            sp.dma_start(wo_raw, wo.rearrange("(k p) n -> p k n", p=P)).then_inc(w_loaded[W_O], 16)
            for n in range(FF // D):
                sp.dma_start(w1_raw[n], w1[:, n * D:(n + 1) * D].rearrange("(k p) n -> p k n", p=P)
                             ).then_inc(w_loaded[W_1 + n], 16)
            for n in range(NJ // KT):
                sp.dma_start(w2_raw[n], w2[n * D:(n + 1) * D, :].rearrange("(k p) n -> p k n", p=P)
                             ).then_inc(w_loaded[W_2 + n], 16)
            for t in range(TT):
                sp.dma_start(x_sb[:, t], x_tiles[t]).then_inc(x_loaded[t], 16)

            def slot(c, par, attn, ff, batch):
                if not isinstance(c, int) or c < NCHUNK - 1:
                    for t in range(TT):
                        sp.wait_ge(x1_set, 4 * c + t + 1)
                        sp.dma_start(x_sb[:, t], x_tiles[4 * c + (TT + t)]).then_inc(x_loaded[t], 16)
                if ff:
                    for t in range(TT):
                        sp.wait_ge(out_set, 4 * c + (t + 1 - TT))
                        sp.dma_start(out_tiles[4 * c + (t - TT)], x1[1 - par][:, t]).then_inc(out_stored[t], 16)

            slots(sp, slot, loads=True)
            for t in range(TT):
                sp.wait_ge(out_stored[t], 16 * NCHUNK)

        @block.gpsimd
        def _(pool):
            nc.gpsimd.memset(ident[:, :], 0.0).then_inc(pool_chain, 1)
            nc.gpsimd.memset(causal[:, :, :], 0.0).then_inc(pool_chain, 1)
            pool.wait_ge(pool_chain, 2)
            nc.gpsimd.affine_select(out=ident[:, :], in_=ident[:, :], compare_op=ALU.not_equal, fill=1.0,
                                    base=0, pattern=[[-1, P]], channel_multiplier=1).then_inc(const_set, 1)
            nc.gpsimd.affine_select(out=causal[:, :, :], in_=causal[:, :, :], compare_op=ALU.is_ge, fill=MASKED,
                                    base=0, pattern=[[0, GH], [-1, SC]], channel_multiplier=1).then_inc(const_set, 1)
            pool.wait_ge(max_ready, 1)
            nc.gpsimd.partition_all_reduce(gmax[:, :], maxima[:, :], P, bass.bass_isa.ReduceOp.max
                                           ).then_inc(gmax_ready, 1)
            pool.wait_ge(const_dve, 2)
            pool.wait_ge(kv_out, KT + BATCH)
            pool.wait_ge(conv_lo, NCONV)
            pool.wait_ge(rows_loaded, 48)

            def rstd_of(c, n):
                pool.wait_ge(ln_ve, 8 * c + n + 1)
                nc.gpsimd.tensor_tensor(rstd[:, n:n + 1], ve[:, n:n + 1], minus_half[:, :], ALU.pow
                                        ).then_inc(ln_rstd, 1)

            def slot(c, par, attn, ff, batch):
                if not attn:
                    return
                for t in range(TT):
                    rstd_of(c, t)
                if batch is not None:
                    wait(pool, v_ps, 4 * c)
                    for a in range(2):
                        keys = kT_sb[:, a, :, bass.ds(batch * SC, SC)]
                        nc.gpsimd.tensor_tensor(
                            kblk[:, a], keys.unsqueeze(2).to_broadcast([P, KT, GH, SC]),
                            mask_k[:, :].unsqueeze(1).unsqueeze(3).to_broadcast([P, KT, GH, SC]),
                            ALU.mult).then_inc(blk_set, 1)
                    for a in range(2):
                        vals = v_sb[:, a, bass.ds(batch, 1), :].rearrange("p b (m n) -> p (b m) n", m=KT)
                        nc.gpsimd.tensor_tensor(
                            vblk[:, a], vals.unsqueeze(2).to_broadcast([P, KT, 2, P]),
                            mask_v[:, :, :].unsqueeze(1).to_broadcast([P, KT, 2, P]),
                            ALU.mult).then_inc(blk_set, 1)
                for t in range(TT):
                    pool.wait_ge(ln_out, 8 * c + t + 1)
                    nc.gpsimd.tensor_tensor(x_sb[:, t], x_sb[:, t], bo_row[:, :], ALU.add).then_inc(xb_set, 1)
                for t in range(TT):
                    pool.wait_ge(s_rec, 4 * c + t + 1)
                    pr = probs[t].rearrange("p (h k) -> p h k", k=SC)
                    nc.gpsimd.tensor_tensor(pr, pr, rsum[:, t, :].unsqueeze(2).to_broadcast([P, HEADS, SC]),
                                            ALU.mult).then_inc(p_norm, 1)

                def add_b2(t):
                    pool.wait_ge(ln_out, 8 * c + (TT + t + 1))
                    nc.gpsimd.tensor_tensor(x1[par][:, t], x1[par][:, t], b2_row[:, :], ALU.add
                                            ).then_inc(x1b_set, 1)
                for t in range(TT):
                    rstd_of(c, TT + t)
                    if t:
                        add_b2(t - 1)
                add_b2(TT - 1)

            slots(pool, slot)

        @block.scalar
        def _(act):
            def convert(n):
                src, scale, hi, lo = conversions[n]
                if n == OVERLAID:
                    act.wait_ge(kv_out, KT + BATCH)
                nc.scalar.activation(hi, src, ACT.Copy, scale=scale).then_inc(conv_hi, 1)

            act.wait_ge(scales_ready, 1)
            for n in range(OVERLAID):
                convert(n)
            for m in range(KT):
                act.wait_ge(kv_ps, m + 1)
                if m >= 2:
                    act.wait_ge(kv_out, m - 1)
                nc.scalar.activation(kv_full[m % 2], ff1_ps[:, m % 2, :], ACT.Identity,
                                     bias=bkp[:, m:m + 1], scale=col(CK)).then_inc(k_full_set, 1)
            for n in range(OVERLAID, NCONV):
                convert(n)
            act.wait_ge(conv_lo, NCONV)

            def slot(c, par, attn, ff, batch):
                for g in range(GROUPS):
                    if ff and g < NJ:
                        act.wait_ge(ff1_done, NJ * c + (g + 1 - NJ))
                        if g >= 2:
                            act.wait_ge(g_lo, NJ * c + (g - 1 - NJ))
                        else:
                            wait(act, g_lo, NJ * c + (-NJ))
                        nc.scalar.activation(gelu_full[g % 2], ff1_ps[:, g % 2, :], ACT.Gelu,
                                             bias=b1p[:, g:g + 1], scale=col(C1)).then_inc(g_full, 1)
                    if not attn:
                        continue
                    for kind, t in PLAN.get(2 * g, []) + PLAN.get(2 * g + 1, []):
                        bank = at_ps[:, t % 2, :]
                        if kind in "TH":
                            done, into, hi = (t_ps, t_hi, aT_hi) if kind == "T" else (h_ps, h_hi, hT[par][:, 0])
                            act.wait_ge(done, 4 * c + t + 1)
                            nc.scalar.activation(hi[:, :, t * P:(t + 1) * P], bank.rearrange("p (k n) -> p k n", k=KT),
                                                 ACT.Copy).then_inc(into, 1)
                        elif kind == "Q":
                            act.wait_ge(q_ps, 4 * c + t + 1)
                            wait(act, q_lo, 4 * c + (t - 1))
                            nc.scalar.activation(q_full[t % 2], bank, ACT.Identity, bias=bqp[:, t:t + 1],
                                                 scale=col(CQ)).then_inc(q_out, 1)
                        elif kind == "E":
                            for u in range(TT):
                                act.wait_ge(s_sub, 4 * c + u + 1)
                                nc.scalar.activation(probs[u], probs[u], ACT.Exp, scale=col(CE)).then_inc(e_set, 1)
                        elif kind == "Z":
                            if t % 2 == 0:
                                wait(act, v_ps, 4 * c + t)
                            for a in range(2):
                                act.wait_ge(z_ps, 8 * c + 2 * t + a + 1)
                                nc.scalar.activation(
                                    pT_hi[:, a * KT:(a + 1) * KT, (t % 2) * P:(t % 2 + 1) * P],
                                    at_ps[:, a, :].rearrange("p (k n) -> p k n", k=KT),
                                    ACT.Copy, scale=PROB_SCALE).then_inc(z_hi, 1)
                        elif kind == "V":
                            act.wait_ge(v_ps, 4 * c + t + 1)
                            nc.scalar.activation(
                                aT_hi[:, 2 * (t % 2):2 * (t % 2) + 2, (t // 2) * HALF:(t // 2 + 1) * HALF],
                                bank.rearrange("p (m n) -> p m n", m=2), ACT.Copy, scale=1.0 / PROB_SCALE
                            ).then_inc(v_hi, 1)

            slots(act, slot)

        @block.vector
        def _(dve):
            links = [0]

            def link(ins):
                links[0] += 1
                ins.then_inc(chain, 1)
                dve.wait_ge(chain, links[0])

            nc.vector.memset(mask_k[:, :].bitcast(F16), 0.0).then_inc(chain, 1)
            nc.vector.memset(mask_v[:, :, :], 0.0).then_inc(chain, 1)
            nc.vector.memset(minus_half[:, :], -0.5).then_inc(chain, 1)
            links[0] += 3
            dve.wait_ge(chain, 3)
            for h in range(GH):
                last = nc.vector.memset(mask_k[HD * h:HD * (h + 1), h:h + 1], 1.0)
            last.then_inc(const_dve, 1)
            for e in range(2):
                for r in range(2):
                    last = nc.vector.memset(mask_v[SC * r:SC * (r + 1), e, 2 * HD * e + HD * r:2 * HD * e + HD * (r + 1)],
                                            1.0)
            last.then_inc(const_dve, 1)
            dve.wait_ge(const_set, 1)
            nc.vector.tensor_copy(ident_bf[:, :], ident[:, :]).then_inc(const_dve, 1)

            dve.wait_ge(cols_ps, 1)
            nc.vector.tensor_copy(cols[:, :], at_ps[:, 0, 0:NV]).then_inc(cols_set, 1)
            dve.wait_ge(cols_set, 1)

            def absmax(n, src, axis=AX_X):
                nc.vector.tensor_reduce(maxima[:, n:n + 1], src, axis, ALU.max, apply_absolute_value=True
                                        ).then_inc(chain, 1)
                links[0] += 1

            absmax(MG1, cols[:, G1:G1 + KT])
            absmax(MG2, cols[:, G2:G2 + KT])
            absmax(MBK, cols[:, BK:BK + KT])
            dve.wait_ge(ctx_loaded, 16)
            absmax(MC, ctx_raw, AX_XY)
            for n, m, src in ((W_K, MK, wk_raw), (W_V, MV, wv_raw), (W_Q, MQ, wq_raw)):
                dve.wait_ge(w_loaded[n], 16)
                absmax(m, src, AX_XY)
            dve.wait_ge(rows_loaded, 48)
            absmax(MBV, bv_row)
            dve.wait_ge(w_loaded[W_O], 16)
            absmax(MO, wo_raw, AX_XY)
            for n in range(FF // D):
                dve.wait_ge(w_loaded[W_1 + n], 16)
                absmax(11 + n, w1_raw[n], AX_XY)
            for n in range(NJ // KT):
                dve.wait_ge(w_loaded[W_2 + n], 16)
                absmax(11 + FF // D + n, w2_raw[n], AX_XY)
            dve.wait_ge(biases_ps, 1)
            link(nc.vector.tensor_tensor(bqp[:, :], at_ps[:, 1, 0:KT], cols[:, BQ:BQ + KT], ALU.add))
            link(nc.vector.tensor_tensor(b1p[:, :], at_ps[:, 1, KT:KT + NJ], cols[:, B1F:B1F + NJ], ALU.add))
            absmax(MBQ, bqp[:, :])
            absmax(MB1, b1p[:, :])
            dve.wait_ge(chain, links[0])
            nc.vector.tensor_scalar(ws[:, 7:8], maxima[:, 0:1], 0.0, None, ALU.mult).then_inc(max_ready, 1)

            dve.wait_ge(gmax_ready, 1)

            def gm(n):
                return gmax[:, n:n + 1]

            def bd(n):
                return bound[:, n:n + 1]

            n1 = FF // D
            link(nc.vector.tensor_scalar(gmax[:, :], gmax[:, :], 1e-18, None, ALU.max))
            link(nc.vector.reduce_max(ws[:, 0:1], gmax[:, 11:11 + n1], AX_X))
            link(nc.vector.reduce_max(bd(L2), gmax[:, 11 + n1:NM], AX_X))
            link(nc.vector.tensor_tensor(bd(LQ), gm(MQ), gm(MG1), ALU.mult))
            link(nc.vector.tensor_tensor(bd(L1), ws[:, 0:1], gm(MG2), ALU.mult))
            for to, frm in ((LK, MK), (LV, MV), (LO, MO), (LC, MC)):
                link(nc.vector.tensor_copy(bd(to), gm(frm)))
            link(nc.vector.scalar_tensor_tensor(bd(LBQ), bd(LQ), LN_BOUND, gm(MBQ), ALU.mult, ALU.add))
            link(nc.vector.scalar_tensor_tensor(bd(LBG), bd(L1), LN_BOUND, gm(MB1), ALU.mult, ALU.add))
            for to, w, b in ((LBK, MK, MBK), (LBV, MV, MBV)):
                link(nc.vector.tensor_scalar(ws[:, 1:2], gm(w), gm(MC), float(D), ALU.mult, ALU.mult))
                link(nc.vector.tensor_tensor(bd(to), ws[:, 1:2], gm(b), ALU.add))
            link(nc.vector.tensor_scalar(pw[:, :].bitcast(I32), bound[:, :].bitcast(I32), 0x7F800000, None,
                                         ALU.bitwise_and))
            link(nc.vector.reciprocal(rp[:, :], pw[:, :]))

            def product(n, factor, *terms):
                first, *rest = terms
                if not rest:
                    link(nc.vector.tensor_scalar(col(n), first, factor, None, ALU.mult))
                    return
                link(nc.vector.tensor_scalar(col(n), first, rest[0], factor, ALU.mult, ALU.mult))
                for r in rest[1:]:
                    link(nc.vector.tensor_scalar(col(n), col(n), r, None, ALU.mult))

            def a(n):
                return pw[:, n:n + 1]

            def r(n):
                return rp[:, n:n + 1]

            for to, n in ((AQ, LQ), (AK, LK), (AV_, LV), (AO, LO), (A1, L1), (A2, L2), (AC, LC)):
                product(to, 2.0 ** 13, r(n))
            for to, n in ((SQ_, LBQ), (SK_, LBK), (SV_, LBV), (SG, LBG)):
                product(to, 2.0 ** 14, r(n))
            product(CQ, 2.0 ** -9, r(LBQ), a(LQ))
            product(CK, 2.0 ** -12, r(LBK), a(LC), a(LK))
            product(CV, 2.0 ** -12, r(LBV), a(LC), a(LV))
            product(CE, 2.0 ** -28 * float(HD) ** -0.5, a(LBQ), a(LBK))
            product(CO, 2.0 ** -27, a(LBV), a(LO))
            product(C1, 2.0 ** -23, a(L1))
            product(C2, 2.0 ** -27, a(LBG), a(L2))
            link(nc.vector.tensor_scalar(gs1[:, :], cols[:, G1:G1 + KT], col(AQ), None, ALU.mult))
            link(nc.vector.tensor_scalar(gs2[:, :], cols[:, G2:G2 + KT], col(A1), None, ALU.mult))
            link(nc.vector.tensor_scalar(bqp[:, :], bqp[:, :], col(SQ_), None, ALU.mult))
            link(nc.vector.tensor_scalar(bkp[:, :], cols[:, BK:BK + KT], col(SK_), None, ALU.mult))
            nc.vector.tensor_scalar(bv_row, bv_row, col(SV_), None, ALU.mult).then_inc(scales_ready, 1)
            dve.wait_ge(scales_ready, 1)

            def convert(n):
                src, scale, hi, lo = conversions[n]
                dve.wait_ge(conv_hi, n + 1)
                if len(src.shape) == 2:
                    nc.vector.scalar_tensor_tensor(lo, src, scale, hi, ALU.mult, ALU.subtract).then_inc(conv_lo, 1)
                else:
                    flat = "p k n -> p (k n)"
                    nc.vector.scalar_tensor_tensor(lo.rearrange(flat), src.rearrange(flat), scale, hi.rearrange(flat),
                                                   ALU.mult, ALU.subtract).then_inc(conv_lo, 1)

            for n in range(OVERLAID):
                convert(n)

            def pair_from(full, hi, lo):
                link(nc.vector.tensor_copy(hi, full))
                nc.vector.tensor_tensor(lo, full, hi, ALU.subtract).then_inc(kv_out, 1)

            for m in range(KT):
                dve.wait_ge(k_full_set, m + 1)
                pair_from(kv_full[m % 2], kT_sb[:, 0, m], kT_sb[:, 1, m])
            for b in range(BATCH):
                dve.wait_ge(kv_ps, KT + b + 1)
                if b == 0:
                    dve.wait_ge(kv_out, KT)
                else:
                    dve.wait_ge(kv_out, KT + b)
                link(nc.vector.scalar_tensor_tensor(kv_full[0], ff1_ps[:, b % 2, :], col(CV), bv_row,
                                                    ALU.mult, ALU.add))
                pair_from(kv_full[0], v_sb[:, 0, b], v_sb[:, 1, b])
            for n in range(OVERLAID, NCONV):
                convert(n)
            dve.wait_ge(conv_lo, NCONV)

            def norm_stats(c, n, src):
                nc.vector.bn_stats(stats[:, n, :], src)
                nc.vector.drain()
                nc.vector.bn_aggr(mv[:, n, :], stats[:, n, :]).then_inc(ln_mv, 1)
                dve.wait_ge(ln_mv, 8 * c + n + 1)
                nc.vector.tensor_scalar(ve[:, n:n + 1], mv[:, n, 1:2], EPS, LN_SCALE ** -2, ALU.add, ALU.mult
                                        ).then_inc(ln_ve, 1)

            def norm_apply(c, n, src):
                dve.wait_ge(ln_rstd, 8 * c + n + 1)
                k = n % TT
                if n < 2:
                    wait(dve, h_ps, 4 * c + (n - 1))
                elif n < TT:
                    dve.wait_ge(t_ps, 4 * c + (n - 1))
                elif k < 2:
                    dve.wait_ge(t_ps, 4 * c + (k + 3))
                else:
                    dve.wait_ge(h_ps, 4 * c + (k - 1))
                nc.vector.tensor_scalar(xhat[:, k % 2, :], src, mv[:, n, 0:1], rstd[:, n:n + 1],
                                        ALU.subtract, ALU.mult).then_inc(ln_out, 1)

            def low(lo, src, factor, hi, done):
                nc.vector.scalar_tensor_tensor(lo, src, factor, hi, ALU.mult, ALU.subtract).then_inc(done, 1)

            def slot(c, par, attn, ff, batch):
                if attn:
                    for t in range(TT):
                        dve.wait_ge(x_loaded[t], 16 * (c + 1))
                        norm_stats(c, t, x_sb[:, t])
                    for t in range(2):
                        norm_apply(c, t, x_sb[:, t])

                def step(kind, t):
                    bank = at_ps[:, t % 2, :]
                    tiles = bank.rearrange("p (k n) -> p k n", k=KT)
                    if kind == "T":
                        dve.wait_ge(t_hi, 4 * c + t + 1)
                        rows = slice(t * P, (t + 1) * P)
                        low(aT_lo[:, :, rows], tiles, 1.0, aT_hi[:, :, rows], t_lo)
                        if t < 2:
                            norm_apply(c, t + 2, x_sb[:, t + 2])
                    elif kind == "H":
                        dve.wait_ge(h_hi, 4 * c + t + 1)
                        rows = slice(t * P, (t + 1) * P)
                        low(hT[par][:, 1, :, rows], tiles, 1.0, hT[par][:, 0, :, rows], h_lo)
                        if t < 2:
                            norm_apply(c, TT + t + 2, x1[par][:, t + 2])
                    elif kind == "Q":
                        dve.wait_ge(q_out, 4 * c + t + 1)
                        nc.vector.tensor_copy(qT_hi[:, t], q_full[t % 2]).then_inc(q_hi, 1)
                        dve.wait_ge(q_hi, 4 * c + t + 1)
                        nc.vector.tensor_tensor(qT_lo[:, t], q_full[t % 2], qT_hi[:, t], ALU.subtract).then_inc(q_lo, 1)
                    elif kind == "S":
                        dve.wait_ge(s_ps, 4 * c + t + 1)
                        nc.vector.tensor_reduce(smax[:, t, :], scores, AX_X, ALU.max).then_inc(s_max, 1)
                        dve.wait_ge(s_max, 4 * c + t + 1)
                        nc.vector.tensor_tensor(probs[t].rearrange("p (h k) -> p h k", k=SC), scores,
                                                smax[:, t, :].unsqueeze(2).to_broadcast([P, HEADS, SC]),
                                                ALU.subtract).then_inc(s_sub, 1)
                    elif kind == "E":
                        for u in range(TT):
                            dve.wait_ge(e_set, 4 * c + u + 1)
                            nc.vector.reduce_sum(ssum[:, u, :], probs[u].rearrange("p (h k) -> p h k", k=SC), AX_X
                                                 ).then_inc(s_sum, 1)
                            dve.wait_ge(s_sum, 4 * c + u + 1)
                            nc.vector.reciprocal(rsum[:, u, :], ssum[:, u, :]).then_inc(s_rec, 1)
                    elif kind == "Z":
                        for a in range(2):
                            dve.wait_ge(z_hi, 8 * c + 2 * t + a + 1)
                            cut = (slice(None), slice(a * KT, (a + 1) * KT), slice((t % 2) * P, (t % 2 + 1) * P))
                            low(pT_lo[cut], at_ps[:, a, :].rearrange("p (k n) -> p k n", k=KT), PROB_SCALE,
                                pT_hi[cut], z_lo)
                    elif kind == "V":
                        dve.wait_ge(v_hi, 4 * c + t + 1)
                        cut = (slice(None), slice(2 * (t % 2), 2 * (t % 2) + 2),
                               slice((t // 2) * HALF, (t // 2 + 1) * HALF))
                        low(aT_lo[cut], bank.rearrange("p (m n) -> p m n", m=2), 1.0 / PROB_SCALE, aT_hi[cut], v_lo)
                    elif kind == "O":
                        dve.wait_ge(o_ps, 4 * c + t + 1)
                        dve.wait_ge(xb_set, 4 * c + t + 1)
                        wait(dve, out_stored[t], 16 * c + (-16))
                        nc.vector.scalar_tensor_tensor(x1[par][:, t], bank, col(CO), x_sb[:, t],
                                                       ALU.mult, ALU.add).then_inc(x1_set, 1)
                        dve.wait_ge(x1_set, 4 * c + t + 1)
                        norm_stats(c, TT + t, x1[par][:, t])
                        if t in (1, 2):
                            norm_apply(c, TT + t - 1, x1[par][:, t - 1])

                for g in range(GROUPS):
                    if attn:
                        for kind, t in PLAN.get(2 * g, []):
                            step(kind, t)
                    if ff and g < NJ:
                        dve.wait_ge(g_full, NJ * c + (g + 1 - NJ))
                        pair = g_pair[g % NG]
                        nc.vector.tensor_scalar(pair[:, 0, :], gelu_full[g % 2], col(SG), None, ALU.mult
                                                ).then_inc(g_hi, 1)
                        dve.wait_ge(g_hi, NJ * c + (g + 1 - NJ))
                        low(pair[:, 1, :], gelu_full[g % 2], col(SG), pair[:, 0, :], g_lo)
                    if attn:
                        for kind, t in PLAN.get(2 * g + 1, []):
                            step(kind, t)
                if ff:
                    for t in range(TT):
                        dve.wait_ge(ff2_done, 4 * c + (t + 1 - TT))
                        if t == 0:
                            dve.wait_ge(x1b_set, 4 * c)
                        old = x1[1 - par][:, t]
                        nc.vector.scalar_tensor_tensor(old, ff2_ps[:, t, :], col(C2), old, ALU.mult, ALU.add
                                                       ).then_inc(out_set, 1)

            slots(dve, slot)

        @block.tensor
        def _(pe):
            def triple(out_ap, pairs):
                last, n = None, 3 * len(pairs)
                i = 0
                for (s_hi, s_lo), (m_hi, m_lo) in pairs:
                    for s, m in ((s_hi, m_hi), (s_hi, m_lo), (s_lo, m_hi)):
                        last = nc.tensor.matmul(out_ap, s, m, start=(i == 0), stop=(i == n - 1))
                        i += 1
                return last

            pe.wait_ge(const_set, 1)
            pe.wait_ge(vecs_loaded, 7 * 16)
            nc.tensor.transpose(at_ps[:, 0, 0:NV], vec_rows[:, :], ident[0:NV, 0:NV]).then_inc(cols_ps, 1)
            pe.wait_ge(ctx_loaded, 16)
            for k in range(KT):
                for n in range(KT):
                    last = nc.tensor.transpose(ff2_ps[:, k, n * P:(n + 1) * P], ctx_raw[:, n, k * P:(k + 1) * P],
                                               ident[:, :])
            last.then_inc(ctxT_ps, 1)
            pe.wait_ge(cols_set, 1)
            pe.wait_ge(w_loaded[W_Q], 16)
            for m in range(KT):
                for k in range(KT):
                    nc.tensor.matmul(at_ps[:, 1, m:m + 1], wq_raw[:, k, m * P:(m + 1) * P],
                                     cols[:, B1LN + k:B1LN + k + 1], start=(k == 0), stop=(k == KT - 1))
            for j in range(NJ):
                if j % KT == 0:
                    pe.wait_ge(w_loaded[W_1 + j // KT], 16)
                for k in range(KT):
                    last = nc.tensor.matmul(at_ps[:, 1, KT + j:KT + j + 1],
                                            w1_raw[j // KT][:, k, (j % KT) * P:(j % KT + 1) * P],
                                            cols[:, B2LN + k:B2LN + k + 1], start=(k == 0), stop=(k == KT - 1))
            last.then_inc(biases_ps, 1)
            pe.wait_ge(conv_lo, KV_CONV)
            for m in range(KT):
                if m >= 2:
                    pe.wait_ge(k_full_set, m - 1)
                cut = slice(m * P, (m + 1) * P)
                triple(ff1_ps[:, m % 2, :], [((wk_hi[:, k, cut], wk_lo[:, k, cut]), (ctxT_hi[:, k], ctxT_lo[:, k]))
                                             for k in range(KT)]).then_inc(kv_ps, 1)
            for b in range(BATCH):
                if b < 2:
                    pe.wait_ge(k_full_set, KT - 1 + b)
                else:
                    pe.wait_ge(kv_out, KT + b - 1)
                cut = slice(b * SC, (b + 1) * SC)
                for r in range(2):
                    last = triple(ff1_ps[r * SC:(r + 1) * SC, b % 2, :],
                                  [((ctxT_hi[:, k, cut], ctxT_lo[:, k, cut]), (wv_hi[:, k], wv_lo[:, k]))
                                   for k in range(KT)])
                last.then_inc(kv_ps, 1)
            pe.wait_ge(conv_lo, NCONV)
            pe.wait_ge(const_set, 2)
            pe.wait_ge(const_dve, 3)

            def slot(c, par, attn, ff, batch):
                def transposes(source, bank, done):
                    for k in range(KT):
                        last = nc.tensor.transpose(at_ps[:, bank, k * P:(k + 1) * P], source[:, k * P:(k + 1) * P],
                                                   ident[:, :])
                    last.then_inc(done, 1)

                def step(kind, t):
                    bank = at_ps[:, t % 2, :]
                    rows = slice(t * P, (t + 1) * P)
                    if kind == "T":
                        pe.wait_ge(ln_out, 8 * c + t + 1)
                        if t < 2:
                            wait(pe, h_lo, 4 * c + (t - 1))
                        else:
                            pe.wait_ge(t_lo, 4 * c + (t - 1))
                        transposes(xhat[:, t % 2, :], t % 2, t_ps)
                    elif kind == "Q":
                        if t == 0:
                            pe.wait_ge(t_lo, 4 * c + 4)
                        elif t >= 2:
                            pe.wait_ge(q_out, 4 * c + (t - 1))
                        triple(bank, [((wq_hi[:, k, rows], wq_lo[:, k, rows]), (aT_hi[:, k], aT_lo[:, k]))
                                      for k in range(KT)]).then_inc(q_ps, 1)
                    elif kind == "S":
                        if t == 0:
                            pe.wait_ge(q_lo, 4 * c + 4)
                            if batch is not None:
                                pe.wait_ge(blk_set, 4 * batch + 4)
                        else:
                            pe.wait_ge(s_sub, 4 * c + t)
                        for g in range(KT):
                            into = at_ps[:, g // 2, (g % 2) * GH * SC:(g % 2 + 1) * GH * SC]
                            kh, kl = (kblk[:, a, g].rearrange("p h k -> p (h k)") for a in range(2))
                            masked = batch is not None and t == 0
                            if masked:
                                nc.tensor.matmul(into, ident_bf[:, :], causal[:, :, :].rearrange("p h k -> p (h k)"),
                                                 start=True, stop=False)
                            for i, (s, m) in enumerate(((qT_hi, kh), (qT_hi, kl), (qT_lo, kh))):
                                last = nc.tensor.matmul(into, s[:, g, rows], m, start=(i == 0 and not masked),
                                                        stop=(i == 2))
                        last.then_inc(s_ps, 1)
                    elif kind == "Z":
                        pe.wait_ge(p_norm, 4 * c + t + 1)
                        for a in range(2):
                            if t == 2:
                                pe.wait_ge(v_lo, 4 * c + a + 1)
                            elif t % 2:
                                pe.wait_ge(z_lo, 8 * c + 2 * t + a - 1)
                            transposes(probs[t][:, a * D:(a + 1) * D], a, z_ps)
                    elif kind == "V":
                        pe.wait_ge(z_lo, 8 * c + 4 * (t // 2 + 1))
                        for i in range(2):
                            m = 2 * (t % 2) + i
                            last = triple(at_ps[:, t % 2, i * HALF:(i + 1) * HALF],
                                          [((vblk[:, 0, m, e], vblk[:, 1, m, e]), (pT_hi[:, 2 * m + e], pT_lo[:, 2 * m + e]))
                                           for e in range(2)])
                        last.then_inc(v_ps, 1)
                    elif kind == "O":
                        if t == 0:
                            pe.wait_ge(v_lo, 4 * c + 4)
                        elif t >= 2:
                            pe.wait_ge(x1_set, 4 * c + (t - 1))
                        triple(bank, [((aT_hi[:, k, rows], aT_lo[:, k, rows]), (wo_hi[:, k], wo_lo[:, k]))
                                      for k in range(KT)]).then_inc(o_ps, 1)
                    elif kind == "H":
                        pe.wait_ge(ln_out, 8 * c + (TT + t + 1))
                        if t < 2:
                            pe.wait_ge(x1_set, 4 * c + (t + 3))
                        else:
                            pe.wait_ge(h_lo, 4 * c + (t - 1))
                        transposes(xhat[:, t % 2, :], t % 2, h_ps)

                old = hT[1 - par]
                for g in range(GROUPS):
                    if ff and g < NJ:
                        if g == 0:
                            pe.wait_ge(h_lo, 4 * c)
                        if g >= 2:
                            pe.wait_ge(g_full, NJ * c + (g - 1 - NJ))
                        else:
                            wait(pe, g_full, NJ * c + (-NJ))
                        cut = slice(g * P, (g + 1) * P)
                        triple(ff1_ps[:, g % 2, :], [((w1_hi[:, k, cut], w1_lo[:, k, cut]), (old[:, 0, k], old[:, 1, k]))
                                                     for k in range(KT)]).then_inc(ff1_done, 1)
                    if attn:
                        for kind, t in PLAN.get(2 * g, []):
                            step(kind, t)
                    if ff and g >= LAG:
                        j = g - LAG
                        pe.wait_ge(g_lo, NJ * c + (j + 1 - NJ))
                        if j == 0:
                            wait(pe, out_set, 4 * c + (-TT))
                        pair = g_pair[j % NG]
                        for t in range(TT):
                            rows = slice(t * P, (t + 1) * P)
                            for i, (s, m) in enumerate(((0, w2_hi), (0, w2_lo), (1, w2_hi))):
                                last = nc.tensor.matmul(ff2_ps[:, t, :], pair[:, s, rows], m[:, j],
                                                        start=(j == 0 and i == 0), stop=(j == NJ - 1 and i == 2))
                            if j == NJ - 1:
                                last.then_inc(ff2_done, 1)
                    if attn:
                        for kind, t in PLAN.get(2 * g + 1, []):
                            step(kind, t)

            slots(pe, slot)


INPUTS = ["x", "ctx_1024"] + ["L0_xattn_" + n for n in (
    "wq", "wk", "wv", "bq", "bk", "bv", "wo", "bo", "ln1_g", "ln1_b", "ln2_g", "ln2_b", "w1", "b1", "w2", "b2")]


def kernel(**inputs):
    import concourse.bacc as bacc
    from concourse.bass_utils import run_bass_kernel_spmd

    nc = bacc.Bacc("TRN2", target_bir_lowering=False, num_devices=1, dynamic_dma_scratch_size=1024)
    arrays, args = {}, []
    for name in INPUTS:
        a = np.ascontiguousarray(inputs[name])
        arrays[f"in_{name}"] = a
        args.append(nc.dram_tensor(f"in_{name}", a.shape, mybir.dt.from_np(a.dtype), kind="ExternalInput").ap())
    out = nc.dram_tensor("out_x", (BATCH, SQ, D), F32, kind="ExternalOutput").ap()
    cross_attention_block(nc, *args, out)
    r = run_bass_kernel_spmd(nc, [arrays], core_ids=[0])
    return r.results[0]["out_x"]
```

```python
from contextlib import ExitStack

import numpy as np

import concourse.bass as bass
from concourse import mybir

F32 = mybir.dt.float32
F16 = mybir.dt.float16
BF16 = mybir.dt.bfloat16
I32 = mybir.dt.int32
ALU = mybir.AluOpType
ACT = mybir.ActivationFunctionType
AX_X = mybir.AxisListType.X
AX_XY = mybir.AxisListType.XY

P = 128
D = 512
KT = D // P
HEADS = 16
HD = D // HEADS
GH = P // HD
BATCH = 8
SQ = 1024
SC = 64
NCTX = BATCH * SC
FF = 2048
NJ = FF // P
CHUNK = 512
TT = CHUNK // P
HALF = CHUNK // 2
NCHUNK = BATCH * SQ // CHUNK
NPAIR = HEADS // 2
EPS = 1e-5
MASKED = -(2.0 ** 120)

LN_SCALE = 2.0 ** 10
PROB_SCALE = 2.0 ** 14
LN_BOUND = D * 22.7

LAG = 2
TINY = 1e-18
CONV_FROM = 17
GROUPS = NJ + LAG
PLAN = {
    2: [("T", 0)], 3: [("T", 1)], 4: [("T", 2)], 5: [("T", 3)],
    6: [("Q", 0)], 7: [("Q", 1)], 8: [("Q", 2)], 9: [("Q", 3)],
    10: [("S", 0)], 12: [("S", 1)], 13: [("S", 2)], 15: [("S", 3)],
    16: [("E", 0)],
    19: [("Z", 0)], 20: [("Z", 1)], 21: [("V", 0), ("V", 1)],
    22: [("Z", 2)], 23: [("Z", 3)], 24: [("V", 2), ("V", 3)],
    25: [("O", 0)], 26: [("O", 1)], 27: [("O", 2)], 28: [("O", 3)],
    30: [("H", 0)], 31: [("H", 1)], 32: [("H", 2)], 33: [("H", 3)],
}


def wait(eng, sem, value):
    if isinstance(value, int) and value <= 0:
        return
    eng.wait_ge(sem, value)


def cross_attention_block(nc, x, context, wq, wk, wv, bq, bk, bv, wo, bo,
                          ln1_g, ln1_b, ln2_g, ln2_b, w1, b1, w2, b2, out):
    x_tiles = x.rearrange("b (n p) d -> (b n) p d", p=P)
    out_tiles = out.rearrange("b (n p) d -> (b n) p d", p=P)
    ctx_rows = context.rearrange("b s d -> (b s) d").rearrange("(n p) d -> p n d", p=P)

    with ExitStack() as ctx:
        def sb(name, shape, dt):
            return ctx.enter_context(nc.sbuf_tensor(name, shape, dt))

        def sem(name):
            return ctx.enter_context(nc.semaphore(name))

        wq_hi, wq_lo = (sb(n, [P, KT, D], F16) for n in ("wq_hi", "wq_lo"))
        wo_hi, wo_lo = (sb(n, [P, KT, D], F16) for n in ("wo_hi", "wo_lo"))
        w1_all = sb("w1_all", [P, 2 * KT * FF], F16)
        w1_hi = w1_all[:, 0:KT * FF].rearrange("p (k n) -> p k n", k=KT)
        w1_lo = w1_all[:, KT * FF:2 * KT * FF].rearrange("p (k n) -> p k n", k=KT)
        w2_all = sb("w2_all", [P, 2 * NJ * D], F16)
        w2_pairs = w2_all[:, :].rearrange("p (k a n) -> p k a n", k=NJ, a=2)
        w2_hi, w2_lo = w2_pairs[:, :, 0], w2_pairs[:, :, 1]
        PIECE = KT * D
        early = [w1_all[:, n * PIECE:(n + 1) * PIECE].rearrange("p (k n) -> p k n", k=KT) for n in range(6)]
        wk_hi, wk_lo, wv_hi, wv_lo, ctxT_hi, ctxT_lo = early
        early_f32 = w1_all[:, 6 * PIECE:].bitcast(F32)
        bv_row = early_f32[:, 0:D]
        kv_full = [early_f32[:, (1 + n) * D:(2 + n) * D] for n in range(2)]
        w1_raw = [w2_all[:, :].bitcast(F32)[:, n * PIECE:(n + 1) * PIECE].rearrange("p (k n) -> p k n", k=KT)
                  for n in range(FF // D)]

        ARENA = 41 * D
        arena = sb("arena", [P, ARENA], F32)
        used = [0]

        def carve(words):
            used[0] += words
            assert used[0] <= ARENA
            return arena[:, used[0] - words:used[0]]

        NG = 4
        q_full = [carve(CHUNK) for _ in range(2)]
        kblk = carve(KT * GH * SC).bitcast(F16).rearrange("p (a g h k) -> p a g h k", a=2, g=KT, h=GH)
        vblk = carve(D).bitcast(F16).rearrange("p (a g n) -> p a g n", a=2, g=NPAIR)
        raw_at = used[0]
        probs = [carve(HEADS * SC) for _ in range(TT)]
        pT = carve(NPAIR * HALF).bitcast(F16).rearrange("p (a g n) -> p a g n", a=2, g=NPAIR)
        pT_hi, pT_lo = pT[:, 0], pT[:, 1]
        x1_a = carve(TT * D)
        hT_a = carve(KT * CHUNK)
        raw2_at = used[0]
        gelu_full = [carve(CHUNK) for _ in range(2)]
        g_pair = [carve(CHUNK).bitcast(F16).rearrange("p (a n) -> p a n", a=2) for _ in range(NG)]
        carve(2 * D)
        x1_b = carve(TT * D)
        hT_b = carve(KT * CHUNK)
        x1 = [v.rearrange("p (t n) -> p t n", t=TT) for v in (x1_a, x1_b)]
        hT = [v.bitcast(F16).rearrange("p (a k n) -> p a k n", a=2, k=KT) for v in (hT_a, hT_b)]

        def raw(at, n):
            return arena[:, at + n * PIECE:at + (n + 1) * PIECE].rearrange("p (k n) -> p k n", k=KT)

        ctx_raw, wk_raw, wv_raw, wq_raw, wo_raw = (raw(raw_at, n) for n in range(5))
        w2_raw = [raw(raw2_at, n) for n in range(NJ // KT)]

        x_sb = sb("x_sb", [P, TT, D], F32)
        xhat = sb("xhat", [P, 2, D], F32)
        act_T = sb("act_T", [P, 2, KT, CHUNK], F16)
        aT_hi, aT_lo = act_T[:, 0], act_T[:, 1]
        qT = sb("qT", [P, 2, KT, CHUNK], F16)
        qT_hi, qT_lo = qT[:, 0], qT[:, 1]
        kT_sb = sb("kT_sb", [P, 2, KT, NCTX], F16)
        v_sb = sb("v_sb", [P, 2, BATCH, D], F16)
        bo_row = sb("bo_row", [P, D], F32)
        b2_row = sb("b2_row", [P, D], F32)
        ident = sb("ident", [P, P], F32)
        ident_bf = sb("ident_bf", [P, P], BF16)
        causal = sb("causal", [P, GH, SC], BF16)
        mask_k = sb("mask_k", [P, GH], F16)
        mask_v = sb("mask_v", [P, 2 * HD], F16)
        N1, N2 = FF // D, NJ // KT
        NV = 6 * KT + NJ
        vec_rows = sb("vec_rows", [NV, P], F32)
        cols = sb("cols", [P, NV], F32)
        BQ, BK, G1, B1LN, G2, B2LN, B1F = (KT * n for n in range(7))
        bqp = sb("bqp", [P, KT], F32)
        bkp = sb("bkp", [P, KT], F32)
        b1p = sb("b1p", [P, NJ], F32)
        gs1 = sb("gs1", [P, KT], F32)
        gs2 = sb("gs2", [P, KT], F32)
        MC, MK, MV, MBK, MBV, MQ, MG1, MBQ, M1, M2, MG2, MB1, MO = (*range(9), 8 + N1, 8 + N1 + N2, 9 + N1 + N2,
                                                                10 + N1 + N2)
        ROUNDS = (slice(MC, MQ), slice(MQ, M1), slice(M1, MO + 1))
        maxima = sb("maxima", [P, MO + 1], F32)
        gmax = sb("gmax", [P, MO + 1], F32)
        LC, LK, LV, LBK, LBV, LQ, LBQ, L1, L2, LO, LBG = range(11)
        bound = sb("bound", [P, 11], F32)
        power = sb("power", [P, 11], F32)
        inverse = sb("inverse", [P, 11], F32)
        tmp = sb("tmp", [P, 2], F32)
        AC, AK, AV, SK, SV, CK, CV, AQ, SQ_, CQ, CE, A1, A2, AO, SG, C1, C2, CO = range(18)
        scales = sb("scales", [P, 18], F32)
        minus_half = sb("minus_half", [P, 1], F32)
        stats = sb("stats", [P, 2 * TT, 6], F32)
        mv = sb("mv", [P, 2 * TT, 2], F32)
        ve = sb("ve", [P, 2 * TT], F32)
        rstd = sb("rstd", [P, 2 * TT], F32)
        smax = sb("smax", [P, TT, HEADS], F32)
        ssum = sb("ssum", [P, TT, HEADS], F32)
        rsum = sb("rsum", [P, TT, HEADS], F32)

        def col(n):
            return scales[:, n:n + 1]

        ff2_ps = ctx.enter_context(nc.psum_tensor("ff2_ps", [P, TT, D], F32))
        ff1_ps = ctx.enter_context(nc.psum_tensor("ff1_ps", [P, 2, CHUNK], F32))
        at_ps = ctx.enter_context(nc.psum_tensor("at_ps", [P, 2, CHUNK], F32))
        scores = at_ps[:, :, :].rearrange("p a (h k) -> p (a h) k", k=SC)

        bias_bank = (at_ps[:, 1, :], ff1_ps[:, 0, :])
        bias_cols = (at_ps[:, 0, :], ff1_ps[:, 1, :])

        NW = 12
        w_loaded = [sem(f"w_loaded{n}") for n in range(NW)]
        W_K, W_V, W_Q, W_O, W_1, W_2 = 0, 1, 2, 3, 4, 8
        ctx_loaded = sem("ctx_loaded")
        vecs_loaded = sem("vecs_loaded")
        bv_loaded = sem("bv_loaded")
        rows_loaded = sem("rows_loaded")
        const_set = sem("const_set")
        const_dve = sem("const_dve")
        cols_ps = sem("cols_ps")
        cols_set = sem("cols_set")
        ctxT_ps = sem("ctxT_ps")
        bias_rows_ps, bias_rows_set, biases_ps = ([sem(f"{n}{i}") for i in range(2)] for n in (
            "bias_rows_ps", "bias_rows_set", "biases_ps"))
        max_ready, gmax_ready, scales_ready = ([sem(f"{n}{i}") for i in range(3)] for n in (
            "max_ready", "gmax_ready", "scales_ready"))
        kv_scales_ready = sem("kv_scales_ready")
        chain = sem("chain")
        pool_chain = sem("pool_chain")
        ctx_hi, ctx_lo = sem("ctx_hi"), sem("ctx_lo")
        conv_hi = sem("conv_hi")
        conv_lo = sem("conv_lo")
        kv_ps = sem("kv_ps")
        k_full_set = sem("k_full_set")
        kv_out = sem("kv_out")
        v_moved = sem("v_moved")
        x_loaded = [sem(f"x_loaded{t}") for t in range(TT)]
        out_stored = [sem(f"out_stored{t}") for t in range(TT)]
        ln_mv, ln_ve, ln_rstd, ln_out = (sem(n) for n in ("ln_mv", "ln_ve", "ln_rstd", "ln_out"))
        xb_set = sem("xb_set")
        x1b_set = sem("x1b_set")
        blk_set = sem("blk_set")
        (t_ps, q_ps, s_ps, z_ps, v_ps, o_ps, h_ps, ff1_done, ff2_done) = (sem(n) for n in (
            "t_ps", "q_ps", "s_ps", "z_ps", "v_ps", "o_ps", "h_ps", "ff1_done", "ff2_done"))
        t_hi, t_lo, q_out, q_hi, q_lo, s_max, s_sub, e_set, s_sum, s_rec, p_norm = (sem(n) for n in (
            "t_hi", "t_lo", "q_out", "q_hi", "q_lo", "s_max", "s_sub", "e_set", "s_sum", "s_rec", "p_norm"))
        z_hi, z_lo, v_hi, v_lo, x1_set, h_hi, h_lo, g_full, g_hi, g_lo, out_set = (sem(n) for n in (
            "z_hi", "z_lo", "v_hi", "v_lo", "x1_set", "h_hi", "h_lo", "g_full", "g_hi", "g_lo", "out_set"))

        ctxT_banks = [ff2_ps[:, k, :] for k in range(KT)]
        conversions = []

        def convert_pieces(raw_w, scale_at, hi, lo, columns=slice(None)):
            for k in range(KT):
                conversions.append((raw_w[:, k], scale_at(k), hi[:, k, columns], lo[:, k, columns]))
            return len(conversions)

        CONV_K = convert_pieces(wk_raw, lambda k: col(AK), wk_hi, wk_lo)
        CONV_V = convert_pieces(wv_raw, lambda k: col(AV), wv_hi, wv_lo)
        CONV_Q = convert_pieces(wq_raw, lambda k: gs1[:, k:k + 1], wq_hi, wq_lo)
        CONV_O = convert_pieces(wo_raw, lambda k: col(AO), wo_hi, wo_lo)
        conv_w1, conv_w2 = [], []
        for half in range(2):
            for n in range(half * N1 // 2, (half + 1) * N1 // 2):
                conv_w1.append(convert_pieces(w1_raw[n], lambda k: gs2[:, k:k + 1], w1_hi, w1_lo,
                                              slice(n * D, (n + 1) * D)))
            for n in range(half * N2 // 2, (half + 1) * N2 // 2):
                conv_w2.append(convert_pieces(w2_raw[n], lambda k: col(A2), w2_hi[:, n * KT:(n + 1) * KT],
                                              w2_lo[:, n * KT:(n + 1) * KT]))
        CONV_FIRST = conv_w2[N2 // 2 - 1]

        def conversions_at(c, position):
            if isinstance(c, int) and c == 0:
                start, end, n0 = CONV_FROM, 2 * GROUPS - 1, CONV_FIRST - CONV_Q
                return [CONV_Q + n for n in range(n0) if start + n * (end - start) // n0 == position]
            if isinstance(c, int) and c == 1 and position < len(conversions) - CONV_FIRST:
                return [CONV_FIRST + position]
            return []

        def plan(c, position):
            return [(kind, t) for kind, t in PLAN.get(position, []) if not (isinstance(c, int) and c == 0 and kind == "T")]

        BIAS_GROUP = 5

        def slots(eng, slot, loads=False):
            slot(0, 0, True, False, 0)
            slot(1, 1, True, True, None)
            with eng.Fori(0, BATCH - 1 - loads) as i:
                slot(2 * i + 2, 0, True, True, i + 1)
                slot(2 * i + 3, 1, True, True, None)
            if loads:
                slot(NCHUNK - 2, 0, True, True, BATCH - 1)
                slot(NCHUNK - 1, 1, True, True, None)
            slot(NCHUNK, 0, False, True, None)

        block = ctx.enter_context(nc.Block())

        @block.sync
        def _(sp):
            row = 0
            for v in (bq, bk, ln1_g, ln1_b, ln2_g, ln2_b, b1):
                n = v.shape[0] // P
                sp.dma_start(vec_rows[row:row + n, :], v.rearrange("(k p) -> k p", p=P)).then_inc(vecs_loaded, 16)
                row += n
            sp.dma_start(ctx_raw, ctx_rows).then_inc(ctx_loaded, 16)
            sp.dma_start(wk_raw, wk.rearrange("(k p) n -> p k n", p=P)).then_inc(w_loaded[W_K], 16)
            sp.dma_start(wv_raw, wv.rearrange("(k p) n -> p k n", p=P)).then_inc(w_loaded[W_V], 16)
            sp.dma_start(bv_row, bv.rearrange("(a n) -> a n", a=1).to_broadcast([P, D])).then_inc(bv_loaded, 16)
            sp.dma_start(wq_raw, wq.rearrange("(k p) n -> p k n", p=P)).then_inc(w_loaded[W_Q], 16)
            for t in range(TT):
                sp.dma_start(x_sb[:, t], x_tiles[t]).then_inc(x_loaded[t], 16)
            for v, dst in ((bo, bo_row[:, :]), (b2, b2_row[:, :])):
                sp.dma_start(dst, v.rearrange("(a n) -> a n", a=1).to_broadcast([P, D])).then_inc(rows_loaded, 16)
            sp.dma_start(wo_raw, wo.rearrange("(k p) n -> p k n", p=P)).then_inc(w_loaded[W_O], 16)
            for n in range(N1):
                sp.dma_start(w1_raw[n], w1[:, n * D:(n + 1) * D].rearrange("(k p) n -> p k n", p=P)
                             ).then_inc(w_loaded[W_1 + n], 16)
            for n in range(N2):
                sp.dma_start(w2_raw[n], w2[n * D:(n + 1) * D, :].rearrange("(k p) n -> p k n", p=P)
                             ).then_inc(w_loaded[W_2 + n], 16)
            sp.wait_ge(kv_out, 2 * KT)
            for a in range(2):
                for half in (slice(0, SC), slice(SC, P)):
                    sp.dma_start(v_sb[half, a, 1::2, :], v_sb[SC:P, a, 0::2, :]).then_inc(v_moved, 16)
            sp.wait_ge(v_moved, 4 * 16)
            for a in range(2):
                sp.dma_start(v_sb[SC:P, a, 0::2, :], v_sb[0:SC, a, 0::2, :]).then_inc(v_moved, 16)

            def slot(c, par, attn, ff, batch):
                if not isinstance(c, int) or c < NCHUNK - 1:
                    for t in range(TT):
                        sp.wait_ge(x1_set, 4 * c + t + 1)
                        sp.dma_start(x_sb[:, t], x_tiles[4 * c + (TT + t)]).then_inc(x_loaded[t], 16)
                if ff:
                    for t in range(TT):
                        sp.wait_ge(out_set, 4 * c + (t + 1 - TT))
                        sp.dma_start(out_tiles[4 * c + (t - TT)], x1[1 - par][:, t]).then_inc(out_stored[t], 16)

            slots(sp, slot, loads=True)
            for t in range(TT):
                sp.wait_ge(out_stored[t], 16 * NCHUNK)

        @block.gpsimd
        def _(pool):
            nc.gpsimd.memset(ident[:, :], 0.0).then_inc(pool_chain, 1)
            nc.gpsimd.memset(causal[:, :, :], 0.0).then_inc(pool_chain, 1)
            pool.wait_ge(pool_chain, 2)
            nc.gpsimd.affine_select(out=ident[:, :], in_=ident[:, :], compare_op=ALU.not_equal, fill=1.0,
                                    base=0, pattern=[[-1, P]], channel_multiplier=1).then_inc(const_set, 1)
            nc.gpsimd.affine_select(out=causal[:, :, :], in_=causal[:, :, :], compare_op=ALU.is_ge, fill=MASKED,
                                    base=0, pattern=[[0, GH], [-1, SC]], channel_multiplier=1).then_inc(const_set, 1)

            def reduce_maxima(n):
                pool.wait_ge(max_ready[n], 1)
                nc.gpsimd.partition_all_reduce(gmax[:, ROUNDS[n]], maxima[:, ROUNDS[n]], P,
                                               bass.bass_isa.ReduceOp.max).then_inc(gmax_ready[n], 1)

            def rstd_of(c, n):
                pool.wait_ge(ln_ve, 8 * c + n + 1)
                nc.gpsimd.tensor_tensor(rstd[:, n:n + 1], ve[:, n:n + 1], minus_half[:, :], ALU.pow
                                        ).then_inc(ln_rstd, 1)

            reduce_maxima(0)
            reduce_maxima(1)
            pool.wait_ge(const_dve, 2)
            for t in range(TT):
                rstd_of(0, t)

            def slot(c, par, attn, ff, batch):
                if not attn:
                    return
                first = isinstance(c, int) and c == 0
                if not first:
                    for t in range(TT):
                        rstd_of(c, t)
                if batch is not None:
                    wait(pool, v_ps, 4 * c)
                    if first:
                        pool.wait_ge(kv_out, KT)
                    for a in range(2):
                        keys = kT_sb[:, a, :, bass.ds(batch * SC, SC)]
                        nc.gpsimd.tensor_tensor(
                            kblk[:, a], keys.unsqueeze(2).to_broadcast([P, KT, GH, SC]),
                            mask_k[:, :].unsqueeze(1).unsqueeze(3).to_broadcast([P, KT, GH, SC]),
                            ALU.mult).then_inc(blk_set, 1)
                    if first:
                        pool.wait_ge(v_moved, 6 * 16)
                    for a in range(2):
                        vals = v_sb[:, a, bass.ds(batch, 1), :].rearrange("p b (g n) -> p (b g) n", g=NPAIR)
                        nc.gpsimd.tensor_tensor(vblk[:, a], vals,
                                                mask_v[:, :].unsqueeze(1).to_broadcast([P, NPAIR, 2 * HD]),
                                                ALU.mult).then_inc(blk_set, 1)
                if first:
                    pool.wait_ge(rows_loaded, 2 * 16)
                for t in range(TT):
                    pool.wait_ge(ln_out, 8 * c + t + 1)
                    nc.gpsimd.tensor_tensor(x_sb[:, t], x_sb[:, t], bo_row[:, :], ALU.add).then_inc(xb_set, 1)
                if first:
                    reduce_maxima(2)
                for t in range(TT):
                    pool.wait_ge(s_rec, 4 * c + t + 1)
                    pr = probs[t].rearrange("p (h k) -> p h k", k=SC)
                    nc.gpsimd.tensor_tensor(pr, pr, rsum[:, t, :].unsqueeze(2).to_broadcast([P, HEADS, SC]),
                                            ALU.mult).then_inc(p_norm, 1)

                def add_b2(t):
                    pool.wait_ge(ln_out, 8 * c + (TT + t + 1))
                    nc.gpsimd.tensor_tensor(x1[par][:, t], x1[par][:, t], b2_row[:, :], ALU.add
                                            ).then_inc(x1b_set, 1)
                for t in range(TT):
                    rstd_of(c, TT + t)
                    if t:
                        add_b2(t - 1)
                add_b2(TT - 1)

            slots(pool, slot)

        @block.scalar
        def _(act):
            def convert(n):
                src, scale, hi, lo = conversions[n]
                for piece, done in enumerate(conv_w2):
                    if n == done - KT:
                        act.wait_ge(conv_lo, conv_w1[piece])
                nc.scalar.activation(hi, src, ACT.Copy, scale=scale).then_inc(conv_hi, 1)

            def bias_rows(n, width, into):
                act.wait_ge(bias_rows_ps[n], 1)
                nc.scalar.activation(into, bias_bank[n][:, 0:width], ACT.Copy).then_inc(bias_rows_set[n], 1)

            act.wait_ge(ctxT_ps, 1)
            act.wait_ge(scales_ready[0], 1)
            for k in range(KT):
                nc.scalar.activation(ctxT_hi[:, k], ctxT_banks[k], ACT.Copy, scale=col(AC)).then_inc(ctx_hi, 1)
                convert(k)
            bias_rows(0, P, q_full[0][:, 0:P])
            for n in range(CONV_K, CONV_V):
                convert(n)
            act.wait_ge(kv_scales_ready, 1)
            for m in range(KT):
                act.wait_ge(kv_ps, m + 1)
                if m >= 2:
                    act.wait_ge(kv_out, m - 1)
                nc.scalar.activation(kv_full[m % 2], ff1_ps[:, m % 2, :], ACT.Identity,
                                     bias=bkp[:, m:m + 1], scale=col(CK)).then_inc(k_full_set, 1)
                if m == 0:
                    act.wait_ge(scales_ready[1], 1)
                convert(CONV_V + m)

            def step(c, par, kind, t):
                bank = at_ps[:, t % 2, :]
                if kind in "TH":
                    done, into, hi = (t_ps, t_hi, aT_hi) if kind == "T" else (h_ps, h_hi, hT[par][:, 0])
                    act.wait_ge(done, 4 * c + t + 1)
                    nc.scalar.activation(hi[:, :, t * P:(t + 1) * P], bank.rearrange("p (k n) -> p k n", k=KT),
                                         ACT.Copy).then_inc(into, 1)
                elif kind == "Q":
                    act.wait_ge(q_ps, 4 * c + t + 1)
                    wait(act, q_lo, 4 * c + (t - 1))
                    nc.scalar.activation(q_full[t % 2], bank, ACT.Identity, bias=bqp[:, t:t + 1],
                                         scale=col(CQ)).then_inc(q_out, 1)
                elif kind == "E":
                    for u in range(TT):
                        act.wait_ge(s_sub, 4 * c + u + 1)
                        nc.scalar.activation(probs[u], probs[u], ACT.Exp, scale=col(CE)).then_inc(e_set, 1)
                elif kind == "Z":
                    if t % 2 == 0:
                        wait(act, v_ps, 4 * c + t)
                    for a in range(2):
                        act.wait_ge(z_ps, 8 * c + 2 * t + a + 1)
                        nc.scalar.activation(
                            pT_hi[:, a * KT:(a + 1) * KT, (t % 2) * P:(t % 2 + 1) * P],
                            at_ps[:, a, :].rearrange("p (k n) -> p k n", k=KT),
                            ACT.Copy, scale=PROB_SCALE).then_inc(z_hi, 1)
                elif kind == "V":
                    act.wait_ge(v_ps, 4 * c + t + 1)
                    nc.scalar.activation(
                        aT_hi[:, 2 * (t % 2):2 * (t % 2) + 2, (t // 2) * HALF:(t // 2 + 1) * HALF],
                        bank.rearrange("p (m n) -> p m n", m=2), ACT.Copy, scale=1.0 / PROB_SCALE
                    ).then_inc(v_hi, 1)

            for t in range(TT):
                step(0, 0, "T", t)

            def slot(c, par, attn, ff, batch):
                first = isinstance(c, int) and c == 0
                for g in range(GROUPS):
                    if first and g == BIAS_GROUP:
                        act.wait_ge(kv_out, 2 * KT)
                        bias_rows(1, D, kv_full[1])
                    if first and 2 * g == CONV_FROM - 1:
                        act.wait_ge(scales_ready[2], 1)
                    if ff and g < NJ:
                        act.wait_ge(ff1_done, NJ * c + (g + 1 - NJ))
                        if g >= 2:
                            act.wait_ge(g_lo, NJ * c + (g - 1 - NJ))
                        else:
                            wait(act, g_lo, NJ * c + (-NJ))
                        if g == 0 and isinstance(c, int) and c == 1:
                            act.wait_ge(conv_lo, CONV_FIRST)
                        nc.scalar.activation(gelu_full[g % 2], ff1_ps[:, g % 2, :], ACT.Gelu,
                                             bias=b1p[:, g:g + 1], scale=col(C1)).then_inc(g_full, 1)
                    for position in (2 * g, 2 * g + 1):
                        if attn:
                            for kind, t in plan(c, position):
                                step(c, par, kind, t)
                        for n in conversions_at(c, position):
                            convert(n)

            slots(act, slot)

        @block.vector
        def _(dve):
            links = [0]

            def link(ins):
                links[0] += 1
                ins.then_inc(chain, 1)
                dve.wait_ge(chain, links[0])

            nc.vector.memset(mask_k[:, :], 0.0).then_inc(chain, 1)
            nc.vector.memset(mask_v[:, :], 0.0).then_inc(chain, 1)
            nc.vector.memset(minus_half[:, :], -0.5).then_inc(chain, 1)
            links[0] += 3
            dve.wait_ge(chain, 3)
            for h in range(GH):
                last = nc.vector.memset(mask_k[HD * h:HD * (h + 1), h:h + 1], 1.0)
            last.then_inc(const_dve, 1)
            for r in range(2):
                last = nc.vector.memset(mask_v[SC * r:SC * (r + 1), HD * r:HD * (r + 1)], 1.0)
            last.then_inc(const_dve, 1)
            dve.wait_ge(const_set, 1)
            nc.vector.tensor_copy(ident_bf[:, :], ident[:, :]).then_inc(const_dve, 1)

            def norm_stats(c, n, src):
                nc.vector.bn_stats(stats[:, n, :], src)
                nc.vector.drain()
                nc.vector.bn_aggr(mv[:, n, :], stats[:, n, :]).then_inc(ln_mv, 1)
                dve.wait_ge(ln_mv, 8 * c + n + 1)
                nc.vector.tensor_scalar(ve[:, n:n + 1], mv[:, n, 1:2], EPS, LN_SCALE ** -2, ALU.add, ALU.mult
                                        ).then_inc(ln_ve, 1)

            def norm_apply(c, n, src):
                dve.wait_ge(ln_rstd, 8 * c + n + 1)
                k = n % TT
                if n < 2:
                    wait(dve, h_ps, 4 * c + (n - 1))
                elif n < TT:
                    dve.wait_ge(t_ps, 4 * c + (n - 1))
                elif k < 2:
                    dve.wait_ge(t_ps, 4 * c + (k + 3))
                else:
                    dve.wait_ge(h_ps, 4 * c + (k - 1))
                nc.vector.tensor_scalar(xhat[:, k % 2, :], src, mv[:, n, 0:1], rstd[:, n:n + 1],
                                        ALU.subtract, ALU.mult).then_inc(ln_out, 1)

            def low(lo, src, factor, hi, done):
                nc.vector.scalar_tensor_tensor(lo, src, factor, hi, ALU.mult, ALU.subtract).then_inc(done, 1)

            def convert(n):
                src, scale, hi, lo = conversions[n]
                dve.wait_ge(conv_hi, n + 1)
                low(lo, src, scale, hi, conv_lo)

            dve.wait_ge(cols_ps, 1)
            nc.vector.tensor_copy(cols[:, :], at_ps[:, 0, 0:NV]).then_inc(cols_set, 1)
            dve.wait_ge(cols_set, 1)

            def absmax(n, src, axis=AX_X, done=None):
                nc.vector.tensor_reduce(maxima[:, n:n + 1], src, axis, ALU.max, apply_absolute_value=True
                                        ).then_inc(done or chain, 1)
                links[0] += done is None

            absmax(MG1, cols[:, G1:G1 + KT])
            absmax(MBK, cols[:, BK:BK + KT])
            absmax(MG2, cols[:, G2:G2 + KT])
            dve.wait_ge(ctx_loaded, 16)
            absmax(MC, ctx_raw, AX_XY)
            dve.wait_ge(w_loaded[W_K], 16)
            absmax(MK, wk_raw, AX_XY)
            dve.wait_ge(w_loaded[W_V], 16)
            absmax(MV, wv_raw, AX_XY)
            dve.wait_ge(bv_loaded, 16)
            absmax(MBV, bv_row, done=max_ready[0])
            dve.wait_ge(w_loaded[W_Q], 16)
            absmax(MQ, wq_raw, AX_XY)

            def bounds(first, last=None):
                return bound[:, first:(first if last is None else last) + 1]

            def a(first, last=None):
                return power[:, first:(first if last is None else last) + 1]

            def r(first, last=None):
                return inverse[:, first:(first if last is None else last) + 1]

            def gm(first, last=None):
                return gmax[:, first:(first if last is None else last) + 1]

            def sc(first, last=None):
                return scales[:, first:(first if last is None else last) + 1]

            def times(out, *terms):
                src, *rest = terms
                if len(rest) == 1:
                    link(nc.vector.tensor_scalar(out, src, rest[0], None, ALU.mult))
                else:
                    link(nc.vector.tensor_scalar(out, src, rest[0], rest[1], ALU.mult, ALU.mult))

            def powers(first, last):
                link(nc.vector.tensor_scalar(a(first, last).bitcast(I32), bounds(first, last).bitcast(I32),
                                             0x7F800000, None, ALU.bitwise_and))
                link(nc.vector.reciprocal(r(first, last), a(first, last)))

            dve.wait_ge(gmax_ready[0], 1)
            link(nc.vector.tensor_scalar(bounds(LC, LV), gm(MC, MV), TINY, None, ALU.max))
            times(tmp[:, :], bounds(LK, LV), bounds(LC), float(D))
            link(nc.vector.tensor_tensor(bounds(LBK, LBV), tmp[:, :], gm(MBK, MBV), ALU.add))
            powers(LC, LBV)
            nc.vector.tensor_scalar(sc(AC, AV), r(LC, LV), 2.0 ** 13, None, ALU.mult).then_inc(scales_ready[0], 1)
            dve.wait_ge(scales_ready[0], 1)
            times(sc(SK, SV), r(LBK, LBV), 2.0 ** 14)
            times(tmp[:, :], r(LBK, LBV), a(LC), 2.0 ** -12)
            link(nc.vector.tensor_tensor(sc(CK, CV), tmp[:, :], a(LK, LV), ALU.mult))
            times(bv_row, bv_row, col(SV))
            nc.vector.tensor_scalar(bkp[:, :], cols[:, BK:BK + KT], col(SK), None, ALU.mult
                                    ).then_inc(kv_scales_ready, 1)
            for k in range(KT):
                dve.wait_ge(ctx_hi, k + 1)
                low(ctxT_lo[:, k], ctxT_banks[k], col(AC), ctxT_hi[:, k], ctx_lo)
                convert(k)
            dve.wait_ge(biases_ps[0], 1)
            link(nc.vector.tensor_tensor(bqp[:, :], bias_cols[0][:, 0:P:P // KT], cols[:, BQ:BQ + KT], ALU.add))
            absmax(MBQ, bqp[:, :], done=max_ready[1])
            for t in range(TT):
                dve.wait_ge(x_loaded[t], 16)
                norm_stats(0, t, x_sb[:, t])
            for n in range(CONV_K, CONV_V):
                convert(n)
            dve.wait_ge(gmax_ready[1], 1)
            link(nc.vector.tensor_scalar(gm(MQ, MG1), gm(MQ, MG1), TINY, None, ALU.max))
            times(bounds(LQ), gm(MQ), gm(MG1))
            link(nc.vector.scalar_tensor_tensor(bounds(LBQ), bounds(LQ), LN_BOUND, gm(MBQ), ALU.mult, ALU.add))
            powers(LQ, LBQ)
            times(sc(AQ), r(LQ), 2.0 ** 13)
            times(gs1[:, :], cols[:, G1:G1 + KT], col(AQ))
            times(sc(SQ_), r(LBQ), 2.0 ** 14)
            times(sc(CQ), r(LBQ), a(LQ), 2.0 ** -9)
            times(sc(CE), a(LBQ), a(LBK), 2.0 ** -28 * float(HD) ** -0.5)
            nc.vector.tensor_scalar(bqp[:, :], bqp[:, :], col(SQ_), None, ALU.mult).then_inc(scales_ready[1], 1)
            for t in range(2):
                norm_apply(0, t, x_sb[:, t])

            def feed_forward_maximum(n):
                dve.wait_ge(w_loaded[W_1 + n], 16)
                absmax(M1 + n, w1_raw[n] if n < N1 else w2_raw[n - N1], AX_XY)

            def output_maximum():
                dve.wait_ge(w_loaded[W_O], 16)
                absmax(MO, wo_raw, AX_XY)

            def feed_forward_bias():
                dve.wait_ge(biases_ps[1], 1)
                link(nc.vector.tensor_tensor(
                    b1p[:, :].rearrange("p (n b) -> p b n", b=KT),
                    bias_cols[1].rearrange("p (b n r) -> p b n r", b=KT, n=N1)[:, :, :, 0],
                    cols[:, B1F:B1F + NJ].rearrange("p (n b) -> p b n", b=KT), ALU.add))
                absmax(MB1, b1p[:, :], done=max_ready[2])

            def feed_forward_scales():
                dve.wait_ge(gmax_ready[2], 1)
                link(nc.vector.reduce_max(tmp[:, 0:1], gm(M1, M2 - 1), AX_X))
                link(nc.vector.reduce_max(bounds(L2), gm(M2, MG2 - 1), AX_X))
                link(nc.vector.tensor_copy(bounds(LO), gm(MO)))
                link(nc.vector.tensor_scalar(bounds(L2, LO), bounds(L2, LO), TINY, None, ALU.max))
                link(nc.vector.tensor_scalar(tmp[:, 0:1], tmp[:, 0:1], TINY, None, ALU.max))
                link(nc.vector.tensor_scalar(tmp[:, 1:2], gm(MG2), TINY, None, ALU.max))
                times(bounds(L1), tmp[:, 0:1], tmp[:, 1:2])
                link(nc.vector.scalar_tensor_tensor(bounds(LBG), bounds(L1), LN_BOUND, gm(MB1), ALU.mult, ALU.add))
                powers(L1, LBG)
                times(sc(A1, AO), r(L1, LO), 2.0 ** 13)
                times(gs2[:, :], cols[:, G2:G2 + KT], col(A1))
                times(sc(SG), r(LBG), 2.0 ** 14)
                times(sc(C1), a(L1), 2.0 ** -23)
                times(sc(C2), a(LBG), a(L2), 2.0 ** -27)
                nc.vector.tensor_scalar(sc(CO), a(LBV), a(LO), 2.0 ** -27, ALU.mult, ALU.mult
                                        ).then_inc(scales_ready[2], 1)
                dve.wait_ge(scales_ready[2], 1)

            def T_step(c, t):
                dve.wait_ge(t_hi, 4 * c + t + 1)
                rows = slice(t * P, (t + 1) * P)
                low(aT_lo[:, :, rows], at_ps[:, t % 2, :].rearrange("p (k n) -> p k n", k=KT), 1.0,
                    aT_hi[:, :, rows], t_lo)
                if t < 2:
                    norm_apply(c, t + 2, x_sb[:, t + 2])

            def pair_from(full, hi, lo):
                link(nc.vector.tensor_copy(hi, full))
                nc.vector.tensor_tensor(lo, full, hi, ALU.subtract).then_inc(kv_out, 1)

            for m in range(KT):
                dve.wait_ge(k_full_set, m + 1)
                pair_from(kv_full[m % 2], kT_sb[:, 0, m], kT_sb[:, 1, m])
                convert(CONV_V + m)
            for n in range(KT):
                dve.wait_ge(kv_ps, KT + n + 1)
                dve.wait_ge(kv_out, KT + n)
                link(nc.vector.scalar_tensor_tensor(kv_full[0], ff1_ps[:, n % 2, :], col(CV), bv_row,
                                                    ALU.mult, ALU.add))
                pair_from(kv_full[0], v_sb[:, 0, 2 * n], v_sb[:, 1, 2 * n])
                T_step(0, n)

            first_slot = {6 + n: [lambda n=n: feed_forward_maximum(n)] for n in range(N1 + N2)}
            first_slot[5] = [output_maximum]
            first_slot[6 + N1 + N2] = [feed_forward_bias]
            first_slot[CONV_FROM - 2] = [feed_forward_scales]

            def aside(c, position):
                if isinstance(c, int) and c == 0:
                    for work in first_slot.get(position, []):
                        work()
                for n in conversions_at(c, position):
                    convert(n)

            def slot(c, par, attn, ff, batch):
                if attn and not (isinstance(c, int) and c == 0):
                    for t in range(TT):
                        dve.wait_ge(x_loaded[t], 16 * (c + 1))
                        norm_stats(c, t, x_sb[:, t])
                    for t in range(2):
                        norm_apply(c, t, x_sb[:, t])

                def step(kind, t):
                    bank = at_ps[:, t % 2, :]
                    tiles = bank.rearrange("p (k n) -> p k n", k=KT)
                    if kind == "T":
                        T_step(c, t)
                    elif kind == "H":
                        dve.wait_ge(h_hi, 4 * c + t + 1)
                        rows = slice(t * P, (t + 1) * P)
                        low(hT[par][:, 1, :, rows], tiles, 1.0, hT[par][:, 0, :, rows], h_lo)
                        if t < 2:
                            norm_apply(c, TT + t + 2, x1[par][:, t + 2])
                    elif kind == "Q":
                        dve.wait_ge(q_out, 4 * c + t + 1)
                        nc.vector.tensor_copy(qT_hi[:, t], q_full[t % 2]).then_inc(q_hi, 1)
                        dve.wait_ge(q_hi, 4 * c + t + 1)
                        nc.vector.tensor_tensor(qT_lo[:, t], q_full[t % 2], qT_hi[:, t], ALU.subtract).then_inc(q_lo, 1)
                    elif kind == "S":
                        dve.wait_ge(s_ps, 4 * c + t + 1)
                        nc.vector.tensor_reduce(smax[:, t, :], scores, AX_X, ALU.max).then_inc(s_max, 1)
                        dve.wait_ge(s_max, 4 * c + t + 1)
                        nc.vector.tensor_tensor(probs[t].rearrange("p (h k) -> p h k", k=SC), scores,
                                                smax[:, t, :].unsqueeze(2).to_broadcast([P, HEADS, SC]),
                                                ALU.subtract).then_inc(s_sub, 1)
                    elif kind == "E":
                        for u in range(TT):
                            dve.wait_ge(e_set, 4 * c + u + 1)
                            nc.vector.reduce_sum(ssum[:, u, :], probs[u].rearrange("p (h k) -> p h k", k=SC), AX_X
                                                 ).then_inc(s_sum, 1)
                            dve.wait_ge(s_sum, 4 * c + u + 1)
                            nc.vector.reciprocal(rsum[:, u, :], ssum[:, u, :]).then_inc(s_rec, 1)
                    elif kind == "Z":
                        for a in range(2):
                            dve.wait_ge(z_hi, 8 * c + 2 * t + a + 1)
                            cut = (slice(None), slice(a * KT, (a + 1) * KT), slice((t % 2) * P, (t % 2 + 1) * P))
                            low(pT_lo[cut], at_ps[:, a, :].rearrange("p (k n) -> p k n", k=KT), PROB_SCALE,
                                pT_hi[cut], z_lo)
                    elif kind == "V":
                        dve.wait_ge(v_hi, 4 * c + t + 1)
                        cut = (slice(None), slice(2 * (t % 2), 2 * (t % 2) + 2),
                               slice((t // 2) * HALF, (t // 2 + 1) * HALF))
                        low(aT_lo[cut], bank.rearrange("p (m n) -> p m n", m=2), 1.0 / PROB_SCALE, aT_hi[cut], v_lo)
                    elif kind == "O":
                        dve.wait_ge(o_ps, 4 * c + t + 1)
                        dve.wait_ge(xb_set, 4 * c + t + 1)
                        wait(dve, out_stored[t], 16 * c + (-16))
                        nc.vector.scalar_tensor_tensor(x1[par][:, t], bank, col(CO), x_sb[:, t],
                                                       ALU.mult, ALU.add).then_inc(x1_set, 1)
                        dve.wait_ge(x1_set, 4 * c + t + 1)
                        norm_stats(c, TT + t, x1[par][:, t])
                        if t in (1, 2):
                            norm_apply(c, TT + t - 1, x1[par][:, t - 1])

                for g in range(GROUPS):
                    if attn:
                        for kind, t in plan(c, 2 * g):
                            step(kind, t)
                    aside(c, 2 * g)
                    if ff and g < NJ:
                        dve.wait_ge(g_full, NJ * c + (g + 1 - NJ))
                        pair = g_pair[g % NG]
                        nc.vector.tensor_scalar(pair[:, 0, :], gelu_full[g % 2], col(SG), None, ALU.mult
                                                ).then_inc(g_hi, 1)
                        dve.wait_ge(g_hi, NJ * c + (g + 1 - NJ))
                        low(pair[:, 1, :], gelu_full[g % 2], col(SG), pair[:, 0, :], g_lo)
                    if attn:
                        for kind, t in plan(c, 2 * g + 1):
                            step(kind, t)
                    aside(c, 2 * g + 1)
                if ff:
                    for t in range(TT):
                        dve.wait_ge(ff2_done, 4 * c + (t + 1 - TT))
                        if t == 0:
                            dve.wait_ge(x1b_set, 4 * c)
                        old = x1[1 - par][:, t]
                        nc.vector.scalar_tensor_tensor(old, ff2_ps[:, t, :], col(C2), old, ALU.mult, ALU.add
                                                       ).then_inc(out_set, 1)

            slots(dve, slot)

        @block.tensor
        def _(pe):
            def triple(out_ap, pairs):
                last, n = None, 3 * len(pairs)
                i = 0
                for (s_hi, s_lo), (m_hi, m_lo) in pairs:
                    for s, m in ((s_hi, m_hi), (s_hi, m_lo), (s_lo, m_hi)):
                        last = nc.tensor.matmul(out_ap, s, m, start=(i == 0), stop=(i == n - 1))
                        i += 1
                return last

            pe.wait_ge(const_set, 1)
            pe.wait_ge(vecs_loaded, 7 * 16)
            nc.tensor.transpose(at_ps[:, 0, 0:NV], vec_rows[:, :], ident[0:NV, 0:NV]).then_inc(cols_ps, 1)
            pe.wait_ge(ctx_loaded, 16)
            for k in range(KT):
                for n in range(KT):
                    last = nc.tensor.transpose(ff2_ps[:, k, n * P:(n + 1) * P], ctx_raw[:, n, k * P:(k + 1) * P],
                                               ident[:, :])
            last.then_inc(ctxT_ps, 1)

            def bias_rows(n, ln_b, weight):
                quarter = P // KT
                for k in range(KT):
                    for m in range(KT):
                        w = weight(k, m)
                        last = nc.tensor.matmul(bias_bank[n][m * quarter:(m + 1) * quarter, 0:w.shape[-1]],
                                                cols[:, ln_b + k:ln_b + k + 1].to_broadcast([P, quarter]), w,
                                                start=(k == 0), stop=(k == KT - 1))
                last.then_inc(bias_rows_ps[n], 1)

            def bias_columns(n, width, rows):
                pe.wait_ge(bias_rows_set[n], 1)
                for b in range(width // P):
                    last = nc.tensor.transpose(bias_cols[n][:, b * P:(b + 1) * P], rows[:, b * P:(b + 1) * P], ident[:, :])
                last.then_inc(biases_ps[n], 1)

            pe.wait_ge(cols_set, 1)
            pe.wait_ge(w_loaded[W_Q], 16)
            bias_rows(0, B1LN, lambda k, m: wq_raw[:, k, m * P:(m + 1) * P])
            bias_columns(0, P, q_full[0])

            def transposes(source, bank, done):
                for k in range(KT):
                    last = nc.tensor.transpose(at_ps[:, bank, k * P:(k + 1) * P], source[:, k * P:(k + 1) * P],
                                               ident[:, :])
                last.then_inc(done, 1)

            def T_step(c, t):
                pe.wait_ge(ln_out, 8 * c + t + 1)
                if t < 2:
                    wait(pe, h_lo, 4 * c + (t - 1))
                else:
                    pe.wait_ge(t_lo, 4 * c + (t - 1))
                transposes(xhat[:, t % 2, :], t % 2, t_ps)

            pe.wait_ge(ctx_lo, KT)
            pe.wait_ge(conv_lo, CONV_K)
            for m in range(KT):
                if m >= 2:
                    pe.wait_ge(k_full_set, m - 1)
                cut = slice(m * P, (m + 1) * P)
                triple(ff1_ps[:, m % 2, :], [((wk_hi[:, k, cut], wk_lo[:, k, cut]), (ctxT_hi[:, k], ctxT_lo[:, k]))
                                             for k in range(KT)]).then_inc(kv_ps, 1)
            pe.wait_ge(conv_lo, CONV_V)
            for n in range(KT):
                if n < 2:
                    pe.wait_ge(k_full_set, KT - 1 + n)
                else:
                    pe.wait_ge(kv_out, KT + n - 1)
                cut = slice(n * P, (n + 1) * P)
                triple(ff1_ps[:, n % 2, :], [((ctxT_hi[:, k, cut], ctxT_lo[:, k, cut]), (wv_hi[:, k], wv_lo[:, k]))
                                             for k in range(KT)]).then_inc(kv_ps, 1)
                T_step(0, n)
            pe.wait_ge(conv_lo, CONV_Q)
            pe.wait_ge(const_set, 2)
            pe.wait_ge(const_dve, 3)

            def slot(c, par, attn, ff, batch):
                def step(kind, t):
                    bank = at_ps[:, t % 2, :]
                    rows = slice(t * P, (t + 1) * P)
                    if kind == "T":
                        T_step(c, t)
                    elif kind == "Q":
                        if t == 0:
                            pe.wait_ge(t_lo, 4 * c + 4)
                        elif t >= 2:
                            pe.wait_ge(q_out, 4 * c + (t - 1))
                        triple(bank, [((wq_hi[:, k, rows], wq_lo[:, k, rows]), (aT_hi[:, k], aT_lo[:, k]))
                                      for k in range(KT)]).then_inc(q_ps, 1)
                    elif kind == "S":
                        if t == 0:
                            pe.wait_ge(q_lo, 4 * c + 4)
                            if batch is not None:
                                pe.wait_ge(blk_set, 4 * batch + 2)
                        else:
                            pe.wait_ge(s_sub, 4 * c + t)
                        for g in range(KT):
                            into = at_ps[:, g // 2, (g % 2) * GH * SC:(g % 2 + 1) * GH * SC]
                            kh, kl = (kblk[:, a, g].rearrange("p h k -> p (h k)") for a in range(2))
                            masked = batch is not None and t == 0
                            if masked:
                                nc.tensor.matmul(into, ident_bf[:, :], causal[:, :, :].rearrange("p h k -> p (h k)"),
                                                 start=True, stop=False)
                            for i, (s, m) in enumerate(((qT_hi, kh), (qT_hi, kl), (qT_lo, kh))):
                                last = nc.tensor.matmul(into, s[:, g, rows], m, start=(i == 0 and not masked),
                                                        stop=(i == 2))
                        last.then_inc(s_ps, 1)
                    elif kind == "Z":
                        pe.wait_ge(p_norm, 4 * c + t + 1)
                        for a in range(2):
                            if t == 2:
                                pe.wait_ge(v_lo, 4 * c + a + 1)
                            elif t % 2:
                                pe.wait_ge(z_lo, 8 * c + 2 * t + a - 1)
                            transposes(probs[t][:, a * D:(a + 1) * D], a, z_ps)
                    elif kind == "V":
                        pe.wait_ge(z_lo, 8 * c + 4 * (t // 2 + 1))
                        if batch is not None:
                            pe.wait_ge(blk_set, 4 * batch + 4)
                        for i in range(2):
                            m = 2 * (t % 2) + i
                            for n, (s, mv_) in enumerate(((0, pT_hi), (0, pT_lo), (1, pT_hi))):
                                for e in range(2):
                                    last = nc.tensor.matmul(
                                        at_ps[SC * e:SC * (e + 1), t % 2, i * HALF:(i + 1) * HALF],
                                        vblk[:, s, 2 * m + e], mv_[:, 2 * m + e], start=(n == 0), stop=(n == 2))
                        last.then_inc(v_ps, 1)
                    elif kind == "O":
                        if t == 0:
                            if isinstance(c, int) and c == 0:
                                pe.wait_ge(conv_lo, CONV_O)
                            pe.wait_ge(v_lo, 4 * c + 4)
                        elif t >= 2:
                            pe.wait_ge(x1_set, 4 * c + (t - 1))
                        triple(bank, [((aT_hi[:, k, rows], aT_lo[:, k, rows]), (wo_hi[:, k], wo_lo[:, k]))
                                      for k in range(KT)]).then_inc(o_ps, 1)
                    elif kind == "H":
                        pe.wait_ge(ln_out, 8 * c + (TT + t + 1))
                        if t < 2:
                            pe.wait_ge(x1_set, 4 * c + (t + 3))
                        else:
                            pe.wait_ge(h_lo, 4 * c + (t - 1))
                        transposes(xhat[:, t % 2, :], t % 2, h_ps)

                old = hT[1 - par]
                for g in range(GROUPS):
                    if isinstance(c, int) and c == 0 and g == BIAS_GROUP:
                        for n in range(N1):
                            pe.wait_ge(w_loaded[W_1 + n], 16)
                        pe.wait_ge(kv_out, 2 * KT)
                        bias_rows(1, B2LN, lambda k, m: w1_raw[m][:, k])
                    if isinstance(c, int) and c == 0 and g == BIAS_GROUP + 1:
                        bias_columns(1, D, kv_full[1])
                    if ff and g < NJ:
                        if g % KT == 0 and isinstance(c, int) and c == 1:
                            pe.wait_ge(conv_lo, conv_w1[g // KT])
                        if g == 0:
                            pe.wait_ge(h_lo, 4 * c)
                        if g >= 2:
                            pe.wait_ge(g_full, NJ * c + (g - 1 - NJ))
                        else:
                            wait(pe, g_full, NJ * c + (-NJ))
                        cut = slice(g * P, (g + 1) * P)
                        triple(ff1_ps[:, g % 2, :], [((w1_hi[:, k, cut], w1_lo[:, k, cut]), (old[:, 0, k], old[:, 1, k]))
                                                     for k in range(KT)]).then_inc(ff1_done, 1)
                    if attn:
                        for kind, t in plan(c, 2 * g):
                            step(kind, t)
                    if ff and g >= LAG:
                        j = g - LAG
                        pe.wait_ge(g_lo, NJ * c + (j + 1 - NJ))
                        if j == 0:
                            wait(pe, out_set, 4 * c + (-TT))
                        if isinstance(c, int) and c == 1:
                            pe.wait_ge(conv_lo, conv_w2[j // KT] - KT + j % KT + 1)
                        pair = g_pair[j % NG]
                        for t in range(TT):
                            rows = slice(t * P, (t + 1) * P)
                            for i, (s, m) in enumerate(((0, w2_hi), (0, w2_lo), (1, w2_hi))):
                                last = nc.tensor.matmul(ff2_ps[:, t, :], pair[:, s, rows], m[:, j],
                                                        start=(j == 0 and i == 0), stop=(j == NJ - 1 and i == 2))
                            if j == NJ - 1:
                                last.then_inc(ff2_done, 1)
                    if attn:
                        for kind, t in plan(c, 2 * g + 1):
                            step(kind, t)

            slots(pe, slot)


INPUTS = ["x", "ctx_1024"] + ["L0_xattn_" + n for n in (
    "wq", "wk", "wv", "bq", "bk", "bv", "wo", "bo", "ln1_g", "ln1_b", "ln2_g", "ln2_b", "w1", "b1", "w2", "b2")]


def kernel(**inputs):
    import concourse.bacc as bacc
    from concourse.bass_utils import run_bass_kernel_spmd

    nc = bacc.Bacc("TRN2", target_bir_lowering=False, num_devices=1, dynamic_dma_scratch_size=1024)
    arrays, args = {}, []
    for name in INPUTS:
        a = np.ascontiguousarray(inputs[name])
        arrays[f"in_{name}"] = a
        args.append(nc.dram_tensor(f"in_{name}", a.shape, mybir.dt.from_np(a.dtype), kind="ExternalInput").ap())
    out = nc.dram_tensor("out_x", (BATCH, SQ, D), F32, kind="ExternalOutput").ap()
    cross_attention_block(nc, *args, out)
    r = run_bass_kernel_spmd(nc, [arrays], core_ids=[0])
    return r.results[0]["out_x"]
```

```python
from contextlib import ExitStack

import numpy as np

import concourse.bass as bass
from concourse import mybir

F32 = mybir.dt.float32
F16 = mybir.dt.float16
BF16 = mybir.dt.bfloat16
I32 = mybir.dt.int32
ALU = mybir.AluOpType
ACT = mybir.ActivationFunctionType
AX_X = mybir.AxisListType.X
AX_XY = mybir.AxisListType.XY

P = 128
D = 512
KT = D // P
HEADS = 16
HD = D // HEADS
GH = P // HD
BATCH = 8
SQ = 1024
SC = 64
NCTX = BATCH * SC
FF = 2048
NJ = FF // P
CHUNK = 512
TT = CHUNK // P
HALF = CHUNK // 2
NCHUNK = BATCH * SQ // CHUNK
NPAIR = HEADS // 2
EPS = 1e-5
MASKED = -(2.0 ** 120)
TINY = 1e-18

LN_SCALE = 2.0 ** 10
PROB_SCALE = 2.0 ** 14
LN_BOUND = D

LAG = 2
GROUPS = NJ + LAG
PLAN = {
    2: [("T", 0)], 4: [("T", 1)], 5: [("T", 2), ("T", 3)],
    6: [("Q", 0)], 7: [("Q", 1)], 8: [("Q", 2)], 9: [("Q", 3)],
    10: [("S", 0)], 12: [("S", 1)], 13: [("S", 2)], 15: [("S", 3)],
    16: [("E", 0), ("E", 1), ("E", 2), ("E", 3)],
    20: [("Z", 0)], 21: [("Z", 1)], 22: [("V", 0), ("V", 1)],
    23: [("Z", 2)], 24: [("Z", 3)], 25: [("V", 2), ("V", 3)],
    26: [("O", 0)], 27: [("O", 1)], 28: [("O", 2)], 29: [("O", 3), ("H", 0)],
    30: [("H", 1)], 31: [("H", 2)], 33: [("H", 3)],
}
PLAN_FIRST = {
    0: [("Q", 0)], 1: [("Q", 1)], 2: [("Q", 2)], 3: [("Q", 3)],
    4: [("S", 0)], 5: [("W", 2)], 6: [("S", 1), ("E", 0)], 7: [("W", 3)],
    8: [("S", 2), ("E", 1)], 9: [("S", 3), ("E", 2)], 10: [("E", 3)],
    12: [("Z", 0)], 13: [("Z", 1)], 14: [("V", 0), ("V", 1)],
    15: [("Z", 2)], 16: [("Z", 3)], 17: [("V", 2), ("V", 3)],
    18: [("O", 0)], 19: [("O", 1)], 20: [("O", 2)], 21: [("O", 3)],
    22: [("H", 0)], 23: [("H", 1)], 24: [("H", 2)], 25: [("H", 3)],
}
W2_SUMS_AT = (0, 1, 20, 21)
BIAS_ROWS_AT, BIAS_COLUMNS_AT = 0, 2
SCALES_AT = 3
CONV_FROM = 12
W2_SCALES_AT = 26
def wait(eng, sem, value):
    if isinstance(value, int) and value <= 0:
        return
    eng.wait_ge(sem, value)


def cross_attention_block(nc, x, context, wq, wk, wv, bq, bk, bv, wo, bo,
                          ln1_g, ln1_b, ln2_g, ln2_b, w1, b1, w2, b2, out):
    x_tiles = x.rearrange("b (n p) d -> (b n) p d", p=P)
    out_tiles = out.rearrange("b (n p) d -> (b n) p d", p=P)
    ctx_rows = context.rearrange("b s d -> (b s) d").rearrange("(n p) d -> p n d", p=P)

    with ExitStack() as ctx:
        def sb(name, shape, dt):
            return ctx.enter_context(nc.sbuf_tensor(name, shape, dt))

        def sem(name):
            return ctx.enter_context(nc.semaphore(name))

        wq_hi, wq_lo = (sb(n, [P, KT, D], F16) for n in ("wq_hi", "wq_lo"))
        wo_hi, wo_lo = (sb(n, [P, KT, D], F16) for n in ("wo_hi", "wo_lo"))
        PIECE = KT * D
        N1, N2 = FF // D, NJ // KT
        w1_all = sb("w1_all", [P, 2 * KT * FF], F16)
        w1_pairs = w1_all[:, :].rearrange("p (n a k m) -> p n a k m", n=N1, a=2, k=KT)
        w2_all = sb("w2_all", [P, 2 * NJ * D], F16)
        w2_pairs = w2_all[:, :].rearrange("p (k a n) -> p k a n", k=NJ, a=2)
        w2_hi, w2_lo = w2_pairs[:, :, 0], w2_pairs[:, :, 1]
        w1_raw = [w2_all[:, :].bitcast(F32)[:, n * PIECE:(n + 1) * PIECE].rearrange("p (k n) -> p k n", k=KT)
                  for n in range(N1)]
        early = [w1_all[:, n * PIECE:(n + 1) * PIECE].rearrange("p (k n) -> p k n", k=KT) for n in range(6)]
        wk_hi, wk_lo, wv_hi, wv_lo, ctxT_hi, ctxT_lo = early
        early_f32 = w1_all[:, 6 * PIECE:].bitcast(F32)
        bv_row = early_f32[:, 0:D]
        kv_full = [early_f32[:, (1 + n) * D:(2 + n) * D] for n in range(2)]
        bias_rows_sb = w1_all[:, 0:2 * D].bitcast(F32)
        w2_raw = [w1_all[:, 2 * n * PIECE:2 * (n + 1) * PIECE].bitcast(F32).rearrange("p (k n) -> p k n", k=KT)
                  for n in range(N1 // 2, N1)]

        ARENA = 39 * D
        arena = sb("arena", [P, ARENA], F32)
        used = [0]

        def carve(words):
            used[0] += words
            assert used[0] <= ARENA
            return arena[:, used[0] - words:used[0]]

        NG = 4
        q_full = [carve(CHUNK) for _ in range(2)]
        kblk = carve(KT * GH * SC).bitcast(F16).rearrange("p (a g h k) -> p a g h k", a=2, g=KT, h=GH)
        vblk = carve(D).bitcast(F16).rearrange("p (a g n) -> p a g n", a=2, g=NPAIR)
        raw_at = used[0]
        probs = [carve(HEADS * SC) for _ in range(TT)]
        pT_words = carve(NPAIR * HALF)
        pT = pT_words.bitcast(F16).rearrange("p (a g n) -> p a g n", a=2, g=NPAIR)
        pT_hi, pT_lo = pT[:, 0], pT[:, 1]
        unused = pT_words[:, 0:PIECE // 2].bitcast(BF16)
        x1_a = carve(TT * D)
        hT_a = carve(KT * CHUNK)
        gelu_full = [carve(CHUNK) for _ in range(2)]
        g_pair = [carve(CHUNK).bitcast(F16).rearrange("p (a n) -> p a n", a=2) for _ in range(NG)]
        raw2_at = used[0]
        x1_b = carve(TT * D)
        hT_b = carve(KT * CHUNK)
        x1 = [v.rearrange("p (t n) -> p t n", t=TT) for v in (x1_a, x1_b)]
        hT = [v.bitcast(F16).rearrange("p (a k n) -> p a k n", a=2, k=KT) for v in (hT_a, hT_b)]

        def raw(at, n):
            return arena[:, at + n * PIECE:at + (n + 1) * PIECE].rearrange("p (k n) -> p k n", k=KT)

        ctx_raw, wk_raw, wv_raw, wq_raw, wo_raw = (raw(raw_at, n) for n in range(5))
        w2_raw += [raw(raw2_at, n) for n in range(N2 // 2)]

        x_sb = sb("x_sb", [P, TT, D], F32)
        xhat = sb("xhat", [P, 2, D], F32)
        act_T = sb("act_T", [P, 2, KT, CHUNK], F16)
        aT_hi, aT_lo = act_T[:, 0], act_T[:, 1]
        qT = sb("qT", [P, 2, KT, CHUNK], F16)
        qT_hi, qT_lo = qT[:, 0], qT[:, 1]
        kT_sb = sb("kT_sb", [P, 2, KT, NCTX], F16)
        v_sb = sb("v_sb", [P, 2, BATCH, D], F16)
        bo_row = sb("bo_row", [P, D], F32)
        b2_row = sb("b2_row", [P, D], F32)
        ident = sb("ident", [P, P], F32)
        ident_bf = sb("ident_bf", [P, P], BF16)
        causal = sb("causal", [P, GH, SC], BF16)
        mask_k = sb("mask_k", [P, GH], F16)
        mask_v = sb("mask_v", [P, 2 * HD], F16)
        W2_ORDER = (2, 3, 0, 1)
        NV = 6 * KT + NJ
        vec_rows = sb("vec_rows", [NV, P], F32)
        cols = sb("cols", [P, NV], F32)
        BQ, BK, G1, B1LN, G2, B2LN, B1F = (KT * n for n in range(7))
        bqp = sb("bqp", [P, KT], F32)
        bkp = sb("bkp", [P, KT], F32)
        b1p = sb("b1p", [P, NJ], F32)
        gs1 = sb("gs1", [P, KT], F32)
        gs2 = sb("gs2", [P, KT], F32)
        MC, MK, MV, MBK, MBV, MQ, MG1, MBQ, MO, MG2, MB1, M1 = range(12)
        M2 = M1 + N1
        ROUNDS = (slice(MC, MQ), slice(MQ, MO), slice(MO, M2), slice(M2, M2 + N2))
        maxima = sb("maxima", [P, M2 + N2], F32)
        gmax = sb("gmax", [P, M2 + N2], F32)
        LC, LK, LV, LBK, LBV, LQ, LBQ, L1, LO, LBG, L2 = range(11)
        bound = sb("bound", [P, 11], F32)
        power = sb("power", [P, 11], F32)
        inverse = sb("inverse", [P, 11], F32)
        tmp = sb("tmp", [P, 2], F32)
        AC, AK, AV, SK, SV, CK, CV, AQ, SQY, CQ, CE, A1, AO, SG, C1, CO, A2, C2 = range(18)
        scales = sb("scales", [P, 18], F32)
        minus_half = sb("minus_half", [P, 1], F32)
        stats = sb("stats", [P, 2 * TT, 6], F32)
        mv = sb("mv", [P, 2 * TT, 2], F32)
        ve = sb("ve", [P, 2 * TT], F32)
        rstd = sb("rstd", [P, 2 * TT], F32)
        smax = sb("smax", [P, TT, HEADS], F32)
        ssum = sb("ssum", [P, TT, HEADS], F32)
        rsum = sb("rsum", [P, TT, HEADS], F32)

        def col(n):
            return scales[:, n:n + 1]

        ff2_ps = ctx.enter_context(nc.psum_tensor("ff2_ps", [P, TT, D], F32))
        ff1_ps = ctx.enter_context(nc.psum_tensor("ff1_ps", [P, 2, CHUNK], F32))
        at_ps = ctx.enter_context(nc.psum_tensor("at_ps", [P, 2, CHUNK], F32))

        bias_bank = (at_ps[:, 1, :], ff1_ps[:, 0, :])
        bias_cols = (at_ps[:, 0, :], ff1_ps[:, 1, :])

        w_loaded = [sem(f"w_loaded{n}") for n in range(4 + N1 + N2)]
        W_K, W_V, W_Q, W_O, W_1, W_2 = 0, 1, 2, 3, 4, 4 + N1
        ctx_loaded = sem("ctx_loaded")
        vecs_loaded = sem("vecs_loaded")
        bv_loaded = sem("bv_loaded")
        rows_loaded = sem("rows_loaded")
        const_set = sem("const_set")
        const_dve = sem("const_dve")
        cols_ps = sem("cols_ps")
        cols_set = sem("cols_set")
        ctxT_ps = sem("ctxT_ps")
        bias_rows_ps, bias_rows_set, biases_ps = ([sem(f"{n}{i}") for i in range(2)] for n in (
            "bias_rows_ps", "bias_rows_set", "biases_ps"))
        max_ready, gmax_ready, scales_ready = ([sem(f"{n}{i}") for i in range(4)] for n in (
            "max_ready", "gmax_ready", "scales_ready"))
        sums_ready = sem("sums_ready")
        kv_scales_ready = sem("kv_scales_ready")
        chain = sem("chain")
        pool_chain = sem("pool_chain")
        ctx_hi, ctx_lo = sem("ctx_hi"), sem("ctx_lo")
        conv_hi = sem("conv_hi")
        conv_lo = sem("conv_lo")
        kv_ps = sem("kv_ps")
        wv_scaled = sem("wv_scaled")
        wv_out = sem("wv_out")
        kv_full_set, kv_hi, kv_out = (sem(n) for n in ("kv_full_set", "kv_hi", "kv_out"))
        v_biased = sem("v_biased")
        v_moved = sem("v_moved")
        x_loaded = [sem(f"x_loaded{t}") for t in range(TT)]
        out_stored = [sem(f"out_stored{t}") for t in range(TT)]
        ln_mv, ln_ve, ln_rstd, ln_out = (sem(n) for n in ("ln_mv", "ln_ve", "ln_rstd", "ln_out"))
        xb_set = sem("xb_set")
        x1b_set = sem("x1b_set")
        blk_set = sem("blk_set")
        (t_ps, q_ps, s_ps, z_ps, v_ps, o_ps, h_ps, ff1_done, ff2_done) = (sem(n) for n in (
            "t_ps", "q_ps", "s_ps", "z_ps", "v_ps", "o_ps", "h_ps", "ff1_done", "ff2_done"))
        t_hi, t_lo, q_out, q_hi, q_lo, s_max, s_sub, e_set, s_sum, s_rec, p_norm = (sem(n) for n in (
            "t_hi", "t_lo", "q_out", "q_hi", "q_lo", "s_max", "s_sub", "e_set", "s_sum", "s_rec", "p_norm"))
        z_hi, z_lo, v_hi, v_lo, x1_set, h_hi, h_lo, g_full, g_hi, g_lo, out_set = (sem(n) for n in (
            "z_hi", "z_lo", "v_hi", "v_lo", "x1_set", "h_hi", "h_lo", "g_full", "g_hi", "g_lo", "out_set"))

        ctxT_banks = [ff2_ps[:, k, :] for k in range(KT)]
        conversions = []

        def convert_pieces(raw_w, scale_at, hi, lo):
            for k in range(KT):
                conversions.append((raw_w[:, k], scale_at(k), hi[:, k], lo[:, k]))
            return len(conversions)

        CONV_K = convert_pieces(wk_raw, lambda k: col(AK), wk_hi, wk_lo)
        CONV_Q = convert_pieces(wq_raw, lambda k: gs1[:, k:k + 1], wq_hi, wq_lo)
        CONV_O = convert_pieces(wo_raw, lambda k: col(AO), wo_hi, wo_lo)
        conv_w1, conv_w2 = {}, {}

        def convert_w1(n):
            conv_w1[n] = convert_pieces(w1_raw[n], lambda k: gs2[:, k:k + 1], w1_pairs[:, n, 0], w1_pairs[:, n, 1])

        def convert_w2(n):
            conv_w2[n] = convert_pieces(w2_raw[n], lambda k: col(A2), w2_hi[:, n * KT:(n + 1) * KT],
                                        w2_lo[:, n * KT:(n + 1) * KT])

        convert_w1(0)
        CONV_FIRST = len(conversions)
        for piece, n in ((convert_w2, 0), (convert_w1, 1), (convert_w1, 2), (convert_w2, 1), (convert_w1, 3),
                         (convert_w2, 2), (convert_w2, 3)):
            piece(n)

        def conversions_at(c, position):
            if isinstance(c, int) and c == 0:
                n = position - CONV_FROM
                return [CONV_Q + n] if 0 <= n < CONV_FIRST - CONV_Q else []
            if isinstance(c, int) and c == 1:
                if position < 4:
                    n = [position - 1] if position else []
                elif position < 7:
                    n = [2 * position - 5, 2 * position - 4]
                else:
                    n = [position + 2]
                return [CONV_FIRST + k for k in n if CONV_FIRST + k < len(conversions)]
            return []

        def plan(c, position):
            return (PLAN_FIRST if isinstance(c, int) and c == 0 else PLAN).get(position, [])

        def halves(c, t):
            return ff2_ps[:, 0:2, :] if isinstance(c, int) and c == 0 and t % 2 else at_ps[:, :, :]

        def slots(eng, slot, loads=False):
            slot(0, 0, True, False, 0)
            slot(1, 1, True, True, None)
            with eng.Fori(0, BATCH - 1 - loads) as i:
                slot(2 * i + 2, 0, True, True, i + 1)
                slot(2 * i + 3, 1, True, True, None)
            if loads:
                slot(NCHUNK - 2, 0, True, True, BATCH - 1)
                slot(NCHUNK - 1, 1, True, True, None)
            slot(NCHUNK, 0, False, True, None)

        block = ctx.enter_context(nc.Block())

        @block.sync
        def _(sp):
            sp.dma_start(ctx_raw, ctx_rows).then_inc(ctx_loaded, 16)
            sp.dma_start(wk_raw, wk.rearrange("(k p) n -> p k n", p=P)).then_inc(w_loaded[W_K], 16)
            row = 0
            for v in (bq, bk, ln1_g, ln1_b, ln2_g, ln2_b, b1):
                n = v.shape[0] // P
                sp.dma_start(vec_rows[row:row + n, :], v.rearrange("(k p) -> k p", p=P)).then_inc(vecs_loaded, 16)
                row += n
            sp.dma_start(wv_raw, wv.rearrange("(k p) n -> p k n", p=P)).then_inc(w_loaded[W_V], 16)
            sp.dma_start(bv_row, bv.rearrange("(a n) -> a n", a=1).to_broadcast([P, D])).then_inc(bv_loaded, 16)
            sp.dma_start(wq_raw, wq.rearrange("(k p) n -> p k n", p=P)).then_inc(w_loaded[W_Q], 16)
            for t in range(TT):
                sp.dma_start(x_sb[:, t], x_tiles[t]).then_inc(x_loaded[t], 16)
            for v, dst in ((bo, bo_row[:, :]), (b2, b2_row[:, :])):
                sp.dma_start(dst, v.rearrange("(a n) -> a n", a=1).to_broadcast([P, D])).then_inc(rows_loaded, 16)
            sp.dma_start(wo_raw, wo.rearrange("(k p) n -> p k n", p=P)).then_inc(w_loaded[W_O], 16)
            for n in range(N1):
                sp.dma_start(w1_raw[n], w1[:, n * D:(n + 1) * D].rearrange("(k p) n -> p k n", p=P)
                             ).then_inc(w_loaded[W_1 + n], 16)

            def load_w2(n):
                sp.dma_start(w2_raw[n], w2[n * D:(n + 1) * D, :].rearrange("(k p) n -> p k n", p=P)
                             ).then_inc(w_loaded[W_2 + n], 16)

            for n in W2_ORDER[:2]:
                load_w2(n)

            def move_values(n, batches):
                even, odd = slice(batches.start, batches.stop, 2), slice(batches.start + 1, batches.stop, 2)
                sp.wait_ge(kv_out, KT + batches.stop // 2)
                for a in range(2):
                    for half in (slice(0, SC), slice(SC, P)):
                        sp.dma_start(v_sb[half, a, odd, :], v_sb[SC:P, a, even, :]).then_inc(v_moved, 16)
                sp.wait_ge(v_moved, (6 * n + 4) * 16)
                for a in range(2):
                    sp.dma_start(v_sb[SC:P, a, even, :], v_sb[0:SC, a, even, :]).then_inc(v_moved, 16)

            move_values(0, slice(0, 2))
            move_values(1, slice(2, BATCH))
            for n in W2_ORDER[2:]:
                load_w2(n)

            def slot(c, par, attn, ff, batch):
                if not isinstance(c, int) or c < NCHUNK - 1:
                    for t in range(TT):
                        sp.wait_ge(x1_set, 4 * c + t + 1)
                        sp.dma_start(x_sb[:, t], x_tiles[4 * c + (TT + t)]).then_inc(x_loaded[t], 16)
                if ff:
                    for t in range(TT):
                        sp.wait_ge(out_set, 4 * c + (t + 1 - TT))
                        sp.dma_start(out_tiles[4 * c + (t - TT)], x1[1 - par][:, t]).then_inc(out_stored[t], 16)

            slots(sp, slot, loads=True)
            for t in range(TT):
                sp.wait_ge(out_stored[t], 16 * NCHUNK)

        @block.gpsimd
        def _(pool):
            nc.gpsimd.memset(ident[:, :], 0.0).then_inc(pool_chain, 1)
            nc.gpsimd.memset(causal[:, :, :], 0.0).then_inc(pool_chain, 1)
            pool.wait_ge(pool_chain, 2)
            nc.gpsimd.affine_select(out=ident[:, :], in_=ident[:, :], compare_op=ALU.not_equal, fill=1.0,
                                    base=0, pattern=[[-1, P]], channel_multiplier=1).then_inc(const_set, 1)
            nc.gpsimd.affine_select(out=causal[:, :, :], in_=causal[:, :, :], compare_op=ALU.is_ge, fill=MASKED,
                                    base=0, pattern=[[0, GH], [-1, SC]], channel_multiplier=1).then_inc(const_set, 1)

            def reduce_maxima(n):
                if n < len(ROUNDS) - 1:
                    pool.wait_ge(max_ready[n], 1)
                nc.gpsimd.partition_all_reduce(gmax[:, ROUNDS[n]], maxima[:, ROUNDS[n]], P,
                                               bass.bass_isa.ReduceOp.max).then_inc(gmax_ready[n], 1)

            def rstd_of(c, n):
                pool.wait_ge(ln_ve, 8 * c + n + 1)
                nc.gpsimd.tensor_tensor(rstd[:, n:n + 1], ve[:, n:n + 1], minus_half[:, :], ALU.pow
                                        ).then_inc(ln_rstd, 1)

            reduce_maxima(0)
            for k in range(KT):
                pool.wait_ge(wv_scaled, k + 1)
                nc.gpsimd.tensor_tensor(wv_lo[:, k], wv_raw[:, k], wv_hi[:, k], ALU.subtract).then_inc(wv_out, 1)
            reduce_maxima(1)
            pool.wait_ge(const_dve, 2)
            for m in range(KT):
                pool.wait_ge(kv_hi, m + 1)
                nc.gpsimd.tensor_tensor(kT_sb[:, 1, m], kv_full[m % 2], kT_sb[:, 0, m], ALU.subtract
                                        ).then_inc(kv_out, 1)
                rstd_of(0, m)

            def values_bias(n):
                pool.wait_ge(kv_full_set, KT + n + 1)
                nc.gpsimd.tensor_tensor(kv_full[n % 2], kv_full[n % 2], bv_row, ALU.add).then_inc(v_biased, 1)

            def values_low(n):
                pool.wait_ge(kv_hi, KT + n + 1)
                nc.gpsimd.tensor_tensor(v_sb[:, 1, 2 * n], kv_full[n % 2], v_sb[:, 0, 2 * n], ALU.subtract
                                        ).then_inc(kv_out, 1)

            for n in range(2):
                values_bias(n)
                values_low(n)

            def slot(c, par, attn, ff, batch):
                if not attn:
                    return
                first = isinstance(c, int) and c == 0
                if not first:
                    for t in range(TT):
                        rstd_of(c, t)

                def key_blocks():
                    for a in range(2):
                        keys = kT_sb[:, a, :, bass.ds(batch * SC, SC)]
                        nc.gpsimd.tensor_tensor(
                            kblk[:, a], keys.unsqueeze(2).to_broadcast([P, KT, GH, SC]),
                            mask_k[:, :].unsqueeze(1).unsqueeze(3).to_broadcast([P, KT, GH, SC]),
                            ALU.mult).then_inc(blk_set, 1)

                def value_blocks():
                    for a in range(2):
                        vals = v_sb[:, a, bass.ds(batch, 1), :].rearrange("p b (g n) -> p (b g) n", g=NPAIR)
                        nc.gpsimd.tensor_tensor(vblk[:, a], vals,
                                                mask_v[:, :].unsqueeze(1).to_broadcast([P, NPAIR, 2 * HD]),
                                                ALU.mult).then_inc(blk_set, 1)

                def add_bo():
                    for t in range(TT):
                        pool.wait_ge(ln_out, 8 * c + t + 1)
                        nc.gpsimd.tensor_tensor(x_sb[:, t], x_sb[:, t], bo_row[:, :], ALU.add).then_inc(xb_set, 1)

                def normalise(t):
                    pool.wait_ge(s_rec, 4 * c + t + 1)
                    pr = probs[t].rearrange("p (h k) -> p h k", k=SC)
                    nc.gpsimd.tensor_tensor(pr, pr, rsum[:, t, :].unsqueeze(2).to_broadcast([P, HEADS, SC]),
                                            ALU.mult).then_inc(p_norm, 1)

                def add_b2(t):
                    pool.wait_ge(ln_out, 8 * c + (TT + t + 1))
                    nc.gpsimd.tensor_tensor(x1[par][:, t], x1[par][:, t], b2_row[:, :], ALU.add
                                            ).then_inc(x1b_set, 1)

                if first:
                    key_blocks()
                    pool.wait_ge(sums_ready, 1)
                    reduce_maxima(2)
                    pool.wait_ge(v_moved, 6 * 16)
                    value_blocks()
                    for n in range(2, KT):
                        values_bias(n)
                        values_low(n)
                    for t in range(TT):
                        normalise(t)
                    pool.wait_ge(v_moved, 12 * 16)
                    pool.wait_ge(rows_loaded, 2 * 16)
                    add_bo()
                    pool.wait_ge(sums_ready, N2 + 1)
                    reduce_maxima(3)
                else:
                    if batch is not None:
                        pool.wait_ge(v_ps, 4 * c)
                        key_blocks()
                        value_blocks()
                    add_bo()
                    for t in range(TT):
                        normalise(t)

                for t in range(TT):
                    rstd_of(c, TT + t)
                    if t:
                        add_b2(t - 1)
                add_b2(TT - 1)

            slots(pool, slot)

        @block.scalar
        def _(act):
            def convert(n):
                src, scale, hi, lo = conversions[n]
                for piece in range(N2):
                    if n == conv_w2[piece] - KT:
                        act.wait_ge(conv_lo, conv_w1[piece])
                    if n == conv_w1[piece] - KT and piece >= N1 // 2:
                        act.wait_ge(conv_lo, conv_w2[piece - N1 // 2])
                nc.scalar.activation(hi, src, ACT.Copy, scale=scale).then_inc(conv_hi, 1)

            def magnitudes(n, sums_before):
                act.wait_ge(w_loaded[n], 16)
                wait(act, sums_ready, sums_before)
                src, column = (wo_raw, MO) if n == W_O else (w2_raw[n - W_2], M2 + n - W_2)
                nc.scalar.activation(unused, src.rearrange("p k n -> p (k n)"), ACT.Abs,
                                     accum_out=maxima[:, column:column + 1]).then_inc(sums_ready, 1)

            def bias_rows(n, width, into):
                act.wait_ge(bias_rows_ps[n], 1)
                nc.scalar.activation(into, bias_bank[n][:, 0:width], ACT.Copy).then_inc(bias_rows_set[n], 1)

            act.wait_ge(ctxT_ps, 1)
            act.wait_ge(scales_ready[0], 1)
            for k in range(KT):
                nc.scalar.activation(ctxT_hi[:, k], ctxT_banks[k], ACT.Copy, scale=col(AC)).then_inc(ctx_hi, 1)
                convert(k)
            bias_rows(0, P, q_full[0][:, 0:P])
            for k in range(KT):
                nc.scalar.activation(wv_hi[:, k], wv_raw[:, k], ACT.Copy, scale=col(AV))
                nc.scalar.activation(wv_raw[:, k], wv_raw[:, k], ACT.Copy, scale=col(AV)).then_inc(wv_scaled, 1)
            act.wait_ge(kv_scales_ready, 1)
            for m in range(KT):
                act.wait_ge(kv_ps, m + 1)
                if m >= 2:
                    act.wait_ge(kv_out, m - 1)
                for into, done in ((kv_full[m % 2], kv_full_set), (kT_sb[:, 0, m], kv_hi)):
                    nc.scalar.activation(into, ff1_ps[:, m % 2, :], ACT.Identity,
                                         bias=bkp[:, m:m + 1], scale=col(CK)).then_inc(done, 1)

            def step(c, par, kind, t):
                bank = at_ps[:, t % 2, :]
                if kind in "TH":
                    if kind == "H" and t == 0 and isinstance(c, int) and c == 1:
                        act.wait_ge(conv_lo, len(conversions))
                    done, into, hi = (t_ps, t_hi, aT_hi) if kind == "T" else (h_ps, h_hi, hT[par][:, 0])
                    act.wait_ge(done, 4 * c + t + 1)
                    nc.scalar.activation(hi[:, :, t * P:(t + 1) * P], bank.rearrange("p (k n) -> p k n", k=KT),
                                         ACT.Copy).then_inc(into, 1)
                elif kind == "Q":
                    act.wait_ge(q_ps, 4 * c + t + 1)
                    wait(act, q_lo, 4 * c + (t - 1))
                    nc.scalar.activation(q_full[t % 2], bank, ACT.Identity, bias=bqp[:, t:t + 1],
                                         scale=col(CQ)).then_inc(q_out, 1)
                elif kind == "W":
                    values_full(t)
                    values_high(t)
                elif kind == "E":
                    act.wait_ge(s_sub, 4 * c + t + 1)
                    nc.scalar.activation(probs[t], probs[t], ACT.Exp, scale=col(CE)).then_inc(e_set, 1)
                elif kind == "Z":
                    if t % 2 == 0:
                        wait(act, v_ps, 4 * c + t)
                    for a in range(2):
                        act.wait_ge(z_ps, 8 * c + 2 * t + a + 1)
                        nc.scalar.activation(
                            pT_hi[:, a * KT:(a + 1) * KT, (t % 2) * P:(t % 2 + 1) * P],
                            halves(c, t)[:, a].rearrange("p (k n) -> p k n", k=KT),
                            ACT.Copy, scale=PROB_SCALE).then_inc(z_hi, 1)
                elif kind == "V":
                    act.wait_ge(v_ps, 4 * c + t + 1)
                    nc.scalar.activation(
                        aT_hi[:, 2 * (t % 2):2 * (t % 2) + 2, (t // 2) * HALF:(t // 2 + 1) * HALF],
                        bank.rearrange("p (m n) -> p m n", m=2), ACT.Copy, scale=1.0 / PROB_SCALE
                    ).then_inc(v_hi, 1)

            def values_full(n):
                act.wait_ge(kv_ps, KT + n + 1)
                act.wait_ge(kv_out, KT + n - 1)
                nc.scalar.activation(kv_full[n % 2], ff1_ps[:, n % 2, :], ACT.Copy, scale=col(CV)
                                     ).then_inc(kv_full_set, 1)

            def values_high(n):
                act.wait_ge(v_biased, n + 1)
                nc.scalar.activation(v_sb[:, 0, 2 * n], kv_full[n % 2], ACT.Copy).then_inc(kv_hi, 1)

            step(0, 0, "T", 0)
            step(0, 0, "T", 1)
            values_full(0)
            act.wait_ge(scales_ready[1], 1)
            for n in range(CONV_K, CONV_Q):
                convert(n)
            values_high(0)
            step(0, 0, "T", 2)
            values_full(1)
            step(0, 0, "T", 3)
            values_high(1)
            magnitudes(W_O, 0)

            def slot(c, par, attn, ff, batch):
                first = isinstance(c, int) and c == 0
                for g in range(GROUPS):
                    if first and 2 * g == BIAS_ROWS_AT:
                        bias_rows(1, D, bias_rows_sb)
                    if first and 2 * g == CONV_FROM:
                        act.wait_ge(scales_ready[2], 1)
                    if ff and g < NJ:
                        act.wait_ge(ff1_done, NJ * c + (g + 1 - NJ))
                        if g >= 2:
                            act.wait_ge(g_lo, NJ * c + (g - 1 - NJ))
                        else:
                            wait(act, g_lo, NJ * c + (-NJ))
                        nc.scalar.activation(gelu_full[g % 2], ff1_ps[:, g % 2, :], ACT.Gelu,
                                             bias=b1p[:, g:g + 1], scale=col(C1)).then_inc(g_full, 1)
                    for position in (2 * g, 2 * g + 1):
                        if attn:
                            for kind, t in plan(c, position):
                                step(c, par, kind, t)
                        for n in conversions_at(c, position):
                            convert(n)
                        if first and position in W2_SUMS_AT:
                            n = W2_SUMS_AT.index(position)
                            magnitudes(W_2 + W2_ORDER[n], n + 1)
                if first:
                    act.wait_ge(scales_ready[3], 1)

            slots(act, slot)

        @block.vector
        def _(dve):
            links = [0]

            def link(ins):
                links[0] += 1
                ins.then_inc(chain, 1)
                dve.wait_ge(chain, links[0])

            nc.vector.memset(mask_k[:, :], 0.0).then_inc(chain, 1)
            nc.vector.memset(mask_v[:, :], 0.0).then_inc(chain, 1)
            nc.vector.memset(minus_half[:, :], -0.5).then_inc(chain, 1)
            links[0] += 3
            dve.wait_ge(chain, 3)
            for h in range(GH):
                last = nc.vector.memset(mask_k[HD * h:HD * (h + 1), h:h + 1], 1.0)
            last.then_inc(const_dve, 1)
            for r in range(2):
                last = nc.vector.memset(mask_v[SC * r:SC * (r + 1), HD * r:HD * (r + 1)], 1.0)
            last.then_inc(const_dve, 1)
            dve.wait_ge(const_set, 1)
            nc.vector.tensor_copy(ident_bf[:, :], ident[:, :]).then_inc(const_dve, 1)

            def norm_stats(c, n, src):
                nc.vector.bn_stats(stats[:, n, :], src)
                nc.vector.drain()
                nc.vector.bn_aggr(mv[:, n, :], stats[:, n, :]).then_inc(ln_mv, 1)
                dve.wait_ge(ln_mv, 8 * c + n + 1)
                nc.vector.tensor_scalar(ve[:, n:n + 1], mv[:, n, 1:2], EPS, LN_SCALE ** -2, ALU.add, ALU.mult
                                        ).then_inc(ln_ve, 1)

            def norm_apply(c, n, src):
                dve.wait_ge(ln_rstd, 8 * c + n + 1)
                k = n % TT
                if n < 2:
                    wait(dve, h_ps, 4 * c + (n - 1))
                elif n < TT:
                    dve.wait_ge(t_ps, 4 * c + (n - 1))
                elif k < 2:
                    dve.wait_ge(t_ps, 4 * c + (k + 3))
                else:
                    dve.wait_ge(h_ps, 4 * c + (k - 1))
                nc.vector.tensor_scalar(xhat[:, k % 2, :], src, mv[:, n, 0:1], rstd[:, n:n + 1],
                                        ALU.subtract, ALU.mult).then_inc(ln_out, 1)

            def low(lo, src, factor, hi, done):
                nc.vector.scalar_tensor_tensor(lo, src, factor, hi, ALU.mult, ALU.subtract).then_inc(done, 1)

            def convert(n):
                src, scale, hi, lo = conversions[n]
                dve.wait_ge(conv_hi, n + 1)
                low(lo, src, scale, hi, conv_lo)

            def absmax(n, src, axis=AX_X, done=None):
                nc.vector.tensor_reduce(maxima[:, n:n + 1], src, axis, ALU.max, apply_absolute_value=True
                                        ).then_inc(done or chain, 1)
                links[0] += done is None

            dve.wait_ge(ctx_loaded, 16)
            absmax(MC, ctx_raw, AX_XY)
            dve.wait_ge(w_loaded[W_K], 16)
            absmax(MK, wk_raw, AX_XY)
            dve.wait_ge(cols_ps, 1)
            nc.vector.tensor_copy(cols[:, :], at_ps[:, 0, 0:NV]).then_inc(cols_set, 1)
            dve.wait_ge(cols_set, 1)
            absmax(MG1, cols[:, G1:G1 + KT])
            absmax(MBK, cols[:, BK:BK + KT])
            absmax(MG2, cols[:, G2:G2 + KT])
            dve.wait_ge(w_loaded[W_V], 16)
            absmax(MV, wv_raw, AX_XY)
            dve.wait_ge(bv_loaded, 16)
            absmax(MBV, bv_row, done=max_ready[0])

            def bounds(first, last=None):
                return bound[:, first:(first if last is None else last) + 1]

            def a(first, last=None):
                return power[:, first:(first if last is None else last) + 1]

            def r(first, last=None):
                return inverse[:, first:(first if last is None else last) + 1]

            def gm(first, last=None):
                return gmax[:, first:(first if last is None else last) + 1]

            def sc(first, last=None):
                return scales[:, first:(first if last is None else last) + 1]

            def times(out, *terms):
                src, *rest = terms
                if len(rest) == 1:
                    link(nc.vector.tensor_scalar(out, src, rest[0], None, ALU.mult))
                else:
                    link(nc.vector.tensor_scalar(out, src, rest[0], rest[1], ALU.mult, ALU.mult))

            def powers(first, last):
                link(nc.vector.tensor_scalar(a(first, last).bitcast(I32), bounds(first, last).bitcast(I32),
                                             0x7F800000, None, ALU.bitwise_and))
                link(nc.vector.reciprocal(r(first, last), a(first, last)))

            dve.wait_ge(gmax_ready[0], 1)
            link(nc.vector.tensor_scalar(bounds(LC, LV), gm(MC, MV), TINY, None, ALU.max))
            times(tmp[:, :], bounds(LK, LV), bounds(LC), float(D))
            link(nc.vector.tensor_tensor(bounds(LBK, LBV), tmp[:, :], gm(MBK, MBV), ALU.add))
            powers(LC, LBV)
            nc.vector.tensor_scalar(sc(AC, AV), r(LC, LV), 2.0 ** 13, None, ALU.mult).then_inc(scales_ready[0], 1)
            dve.wait_ge(scales_ready[0], 1)
            times(sc(SK, SV), r(LBK, LBV), 2.0 ** 14)
            times(tmp[:, :], r(LBK, LBV), a(LC), 2.0 ** -12)
            link(nc.vector.tensor_tensor(sc(CK, CV), tmp[:, :], a(LK, LV), ALU.mult))
            times(bv_row, bv_row, col(SV))
            nc.vector.tensor_scalar(bkp[:, :], cols[:, BK:BK + KT], col(SK), None, ALU.mult
                                    ).then_inc(kv_scales_ready, 1)
            for k in range(KT):
                dve.wait_ge(ctx_hi, k + 1)
                low(ctxT_lo[:, k], ctxT_banks[k], col(AC), ctxT_hi[:, k], ctx_lo)
                convert(k)

            def query_bias():
                dve.wait_ge(w_loaded[W_Q], 16)
                absmax(MQ, wq_raw, AX_XY)
                dve.wait_ge(biases_ps[0], 1)
                link(nc.vector.tensor_tensor(bqp[:, :], bias_cols[0][:, 0:P:P // KT], cols[:, BQ:BQ + KT], ALU.add))
                absmax(MBQ, bqp[:, :], done=max_ready[1])

            def first_stats(t):
                dve.wait_ge(x_loaded[t], 16)
                norm_stats(0, t, x_sb[:, t])

            def query_scales():
                dve.wait_ge(gmax_ready[1], 1)
                link(nc.vector.tensor_scalar(gm(MQ, MG1), gm(MQ, MG1), TINY, None, ALU.max))
                times(bounds(LQ), gm(MQ), gm(MG1))
                link(nc.vector.scalar_tensor_tensor(bounds(LBQ), bounds(LQ), LN_BOUND, gm(MBQ), ALU.mult, ALU.add))
                powers(LQ, LBQ)
                times(sc(AQ), r(LQ), 2.0 ** 13)
                times(gs1[:, :], cols[:, G1:G1 + KT], col(AQ))
                times(sc(SQY), r(LBQ), 2.0 ** 14)
                times(sc(CQ), r(LBQ), a(LQ), 2.0 ** -9)
                times(sc(CE), a(LBQ), a(LBK), 2.0 ** -28 * float(HD) ** -0.5)
                nc.vector.tensor_scalar(bqp[:, :], bqp[:, :], col(SQY), None, ALU.mult).then_inc(scales_ready[1], 1)

            query_bias()
            for t in range(TT):
                first_stats(t)
            query_scales()
            for t in range(2):
                norm_apply(0, t, x_sb[:, t])

            def feed_forward_maximum(n):
                dve.wait_ge(w_loaded[W_1 + n], 16)
                absmax(M1 + n, w1_raw[n], AX_XY)

            def feed_forward_bias():
                dve.wait_ge(biases_ps[1], 1)
                link(nc.vector.tensor_tensor(
                    b1p[:, :].rearrange("p (n b) -> p b n", b=KT),
                    bias_cols[1].rearrange("p (b n r) -> p b n r", b=KT, n=N1)[:, :, :, 0],
                    cols[:, B1F:B1F + NJ].rearrange("p (n b) -> p b n", b=KT), ALU.add))
                absmax(MB1, b1p[:, :], done=max_ready[2])

            def feed_forward_scales():
                dve.wait_ge(gmax_ready[2], 1)
                link(nc.vector.reduce_max(tmp[:, 0:1], gm(M1, M2 - 1), AX_X))
                link(nc.vector.tensor_scalar(tmp[:, 0:1], tmp[:, 0:1], TINY, None, ALU.max))
                link(nc.vector.tensor_scalar(tmp[:, 1:2], gm(MG2), TINY, None, ALU.max))
                link(nc.vector.tensor_scalar(bounds(LO), gm(MO), TINY, None, ALU.max))
                times(bounds(L1), tmp[:, 0:1], tmp[:, 1:2])
                link(nc.vector.scalar_tensor_tensor(bounds(LBG), bounds(L1), LN_BOUND, gm(MB1), ALU.mult, ALU.add))
                powers(L1, LBG)
                times(sc(A1, AO), r(L1, LO), 2.0 ** 13)
                times(gs2[:, :], cols[:, G2:G2 + KT], col(A1))
                times(sc(SG), r(LBG), 2.0 ** 14)
                times(sc(C1), a(L1), 2.0 ** -23)
                nc.vector.tensor_scalar(sc(CO), a(LBV), a(LO), 2.0 ** -27, ALU.mult, ALU.mult
                                        ).then_inc(scales_ready[2], 1)
                dve.wait_ge(scales_ready[2], 1)

            def w2_scales():
                dve.wait_ge(gmax_ready[3], 1)
                link(nc.vector.reduce_max(bounds(L2), gm(M2, M2 + N2 - 1), AX_X))
                link(nc.vector.tensor_scalar(bounds(L2), bounds(L2), TINY, None, ALU.max))
                powers(L2, L2)
                times(sc(C2), a(LBG), a(L2), 2.0 ** -27)
                nc.vector.tensor_scalar(sc(A2), r(L2), 2.0 ** 13, None, ALU.mult).then_inc(scales_ready[3], 1)
                dve.wait_ge(scales_ready[3], 1)

            def T_step(c, t):
                dve.wait_ge(t_hi, 4 * c + t + 1)
                rows = slice(t * P, (t + 1) * P)
                low(aT_lo[:, :, rows], at_ps[:, t % 2, :].rearrange("p (k n) -> p k n", k=KT), 1.0,
                    aT_hi[:, :, rows], t_lo)
                if t < 2:
                    norm_apply(c, t + 2, x_sb[:, t + 2])

            T_step(0, 0)
            T_step(0, 1)
            for n in range(CONV_K, CONV_Q):
                convert(n)
            T_step(0, 2)
            T_step(0, 3)
            for n in range(N1 // 2):
                feed_forward_maximum(n)

            def aside(c, position):
                if isinstance(c, int) and c == 0:
                    if position < N1 - N1 // 2:
                        feed_forward_maximum(N1 // 2 + position)
                    if position == BIAS_COLUMNS_AT:
                        feed_forward_bias()
                    if position == SCALES_AT:
                        feed_forward_scales()
                    if position == W2_SCALES_AT:
                        w2_scales()
                for n in conversions_at(c, position):
                    convert(n)

            def slot(c, par, attn, ff, batch):
                if attn and not (isinstance(c, int) and c == 0):
                    for t in range(TT):
                        dve.wait_ge(x_loaded[t], 16 * (c + 1))
                        norm_stats(c, t, x_sb[:, t])
                        if t >= 2:
                            norm_apply(c, t - 2, x_sb[:, t - 2])

                def step(kind, t):
                    bank = at_ps[:, t % 2, :]
                    tiles = bank.rearrange("p (k n) -> p k n", k=KT)
                    if kind == "T":
                        T_step(c, t)
                    elif kind == "H":
                        dve.wait_ge(h_hi, 4 * c + t + 1)
                        rows = slice(t * P, (t + 1) * P)
                        low(hT[par][:, 1, :, rows], tiles, 1.0, hT[par][:, 0, :, rows], h_lo)
                        if t < 2:
                            norm_apply(c, TT + t + 2, x1[par][:, t + 2])
                    elif kind == "Q":
                        dve.wait_ge(q_out, 4 * c + t + 1)
                        nc.vector.tensor_copy(qT_hi[:, t], q_full[t % 2]).then_inc(q_hi, 1)
                        dve.wait_ge(q_hi, 4 * c + t + 1)
                        nc.vector.tensor_tensor(qT_lo[:, t], q_full[t % 2], qT_hi[:, t], ALU.subtract).then_inc(q_lo, 1)
                    elif kind == "S":
                        dve.wait_ge(s_ps, 4 * c + t + 1)
                        scores = halves(c, t).rearrange("p a (h k) -> p (a h) k", k=SC)
                        nc.vector.tensor_reduce(smax[:, t, :], scores, AX_X, ALU.max).then_inc(s_max, 1)
                        dve.wait_ge(s_max, 4 * c + t + 1)
                        nc.vector.tensor_tensor(probs[t].rearrange("p (h k) -> p h k", k=SC), scores,
                                                smax[:, t, :].unsqueeze(2).to_broadcast([P, HEADS, SC]),
                                                ALU.subtract).then_inc(s_sub, 1)
                    elif kind == "E":
                        dve.wait_ge(e_set, 4 * c + t + 1)
                        nc.vector.reduce_sum(ssum[:, t, :], probs[t].rearrange("p (h k) -> p h k", k=SC), AX_X
                                             ).then_inc(s_sum, 1)
                        dve.wait_ge(s_sum, 4 * c + t + 1)
                        nc.vector.reciprocal(rsum[:, t, :], ssum[:, t, :]).then_inc(s_rec, 1)
                    elif kind == "Z":
                        for a in range(2):
                            dve.wait_ge(z_hi, 8 * c + 2 * t + a + 1)
                            cut = (slice(None), slice(a * KT, (a + 1) * KT), slice((t % 2) * P, (t % 2 + 1) * P))
                            low(pT_lo[cut], halves(c, t)[:, a].rearrange("p (k n) -> p k n", k=KT), PROB_SCALE,
                                pT_hi[cut], z_lo)
                    elif kind == "V":
                        dve.wait_ge(v_hi, 4 * c + t + 1)
                        cut = (slice(None), slice(2 * (t % 2), 2 * (t % 2) + 2),
                               slice((t // 2) * HALF, (t // 2 + 1) * HALF))
                        low(aT_lo[cut], bank.rearrange("p (m n) -> p m n", m=2), 1.0 / PROB_SCALE, aT_hi[cut], v_lo)
                    elif kind == "O":
                        dve.wait_ge(o_ps, 4 * c + t + 1)
                        dve.wait_ge(xb_set, 4 * c + t + 1)
                        wait(dve, out_stored[t], 16 * c + (-16))
                        nc.vector.scalar_tensor_tensor(x1[par][:, t], bank, col(CO), x_sb[:, t],
                                                       ALU.mult, ALU.add).then_inc(x1_set, 1)
                        dve.wait_ge(x1_set, 4 * c + t + 1)
                        norm_stats(c, TT + t, x1[par][:, t])
                        if t in (1, 2):
                            norm_apply(c, TT + t - 1, x1[par][:, t - 1])

                for g in range(GROUPS):
                    if attn:
                        for kind, t in plan(c, 2 * g):
                            step(kind, t)
                    aside(c, 2 * g)
                    if ff and g < NJ:
                        dve.wait_ge(g_full, NJ * c + (g + 1 - NJ))
                        pair = g_pair[g % NG]
                        nc.vector.tensor_scalar(pair[:, 0, :], gelu_full[g % 2], col(SG), None, ALU.mult
                                                ).then_inc(g_hi, 1)
                        dve.wait_ge(g_hi, NJ * c + (g + 1 - NJ))
                        low(pair[:, 1, :], gelu_full[g % 2], col(SG), pair[:, 0, :], g_lo)
                    if attn:
                        for kind, t in plan(c, 2 * g + 1):
                            step(kind, t)
                    aside(c, 2 * g + 1)
                if ff:
                    for t in range(TT):
                        dve.wait_ge(ff2_done, 4 * c + (t + 1 - TT))
                        if t == 0:
                            dve.wait_ge(x1b_set, 4 * c)
                        old = x1[1 - par][:, t]
                        nc.vector.scalar_tensor_tensor(old, ff2_ps[:, t, :], col(C2), old, ALU.mult, ALU.add
                                                       ).then_inc(out_set, 1)

            slots(dve, slot)

        @block.tensor
        def _(pe):
            def triple(out_ap, pairs):
                last, n = None, 3 * len(pairs)
                i = 0
                for (s_hi, s_lo), (m_hi, m_lo) in pairs:
                    for s, m in ((s_hi, m_hi), (s_hi, m_lo), (s_lo, m_hi)):
                        last = nc.tensor.matmul(out_ap, s, m, start=(i == 0), stop=(i == n - 1))
                        i += 1
                return last

            pe.wait_ge(const_set, 1)
            pe.wait_ge(ctx_loaded, 16)
            for k in range(KT):
                for n in range(KT):
                    last = nc.tensor.transpose(ff2_ps[:, k, n * P:(n + 1) * P], ctx_raw[:, n, k * P:(k + 1) * P],
                                               ident[:, :])
            last.then_inc(ctxT_ps, 1)
            pe.wait_ge(vecs_loaded, 7 * 16)
            nc.tensor.transpose(at_ps[:, 0, 0:NV], vec_rows[:, :], ident[0:NV, 0:NV]).then_inc(cols_ps, 1)

            def bias_rows(n, ln_b, weight):
                quarter = P // KT
                for k in range(KT):
                    for m in range(KT):
                        w = weight(k, m)
                        last = nc.tensor.matmul(bias_bank[n][m * quarter:(m + 1) * quarter, 0:w.shape[-1]],
                                                cols[:, ln_b + k:ln_b + k + 1].to_broadcast([P, quarter]), w,
                                                start=(k == 0), stop=(k == KT - 1))
                last.then_inc(bias_rows_ps[n], 1)

            def bias_columns(n, width, rows):
                pe.wait_ge(bias_rows_set[n], 1)
                for b in range(width // P):
                    last = nc.tensor.transpose(bias_cols[n][:, b * P:(b + 1) * P], rows[:, b * P:(b + 1) * P],
                                               ident[:, :])
                last.then_inc(biases_ps[n], 1)

            pe.wait_ge(cols_set, 1)
            pe.wait_ge(w_loaded[W_Q], 16)
            bias_rows(0, B1LN, lambda k, m: wq_raw[:, k, m * P:(m + 1) * P])
            bias_columns(0, P, q_full[0])

            def transposes(source, bank, done):
                for k in range(KT):
                    last = nc.tensor.transpose(bank[:, k * P:(k + 1) * P], source[:, k * P:(k + 1) * P],
                                               ident[:, :])
                last.then_inc(done, 1)

            def T_step(c, t):
                pe.wait_ge(ln_out, 8 * c + t + 1)
                if t < 2:
                    wait(pe, h_lo, 4 * c + (t - 1))
                else:
                    pe.wait_ge(t_lo, 4 * c + (t - 1))
                transposes(xhat[:, t % 2, :], at_ps[:, t % 2, :], t_ps)

            pe.wait_ge(ctx_lo, KT)
            pe.wait_ge(conv_lo, CONV_K)
            for m in range(KT):
                if m >= 2:
                    pe.wait_ge(kv_hi, m - 1)
                cut = slice(m * P, (m + 1) * P)
                triple(ff1_ps[:, m % 2, :], [((wk_hi[:, k, cut], wk_lo[:, k, cut]), (ctxT_hi[:, k], ctxT_lo[:, k]))
                                             for k in range(KT)]).then_inc(kv_ps, 1)
            for t in range(2):
                T_step(0, t)
            pe.wait_ge(wv_out, KT)

            def values(n):
                if n < 2:
                    pe.wait_ge(kv_hi, KT - 1 + n)
                elif n == 2:
                    pe.wait_ge(bias_rows_set[1], 1)
                elif n == 3:
                    pe.wait_ge(max_ready[2], 1)
                cut = slice(n * P, (n + 1) * P)
                triple(ff1_ps[:, n % 2, :], [((ctxT_hi[:, k, cut], ctxT_lo[:, k, cut]), (wv_hi[:, k], wv_lo[:, k]))
                                             for k in range(KT)]).then_inc(kv_ps, 1)

            for t in range(2, TT):
                values(t - 2)
                T_step(0, t)
            pe.wait_ge(conv_lo, CONV_Q)
            pe.wait_ge(const_set, 2)
            pe.wait_ge(const_dve, 3)

            def slot(c, par, attn, ff, batch):
                def step(kind, t):
                    bank = at_ps[:, t % 2, :]
                    rows = slice(t * P, (t + 1) * P)
                    if kind == "T":
                        T_step(c, t)
                    elif kind == "W":
                        values(t)
                    elif kind == "Q":
                        if t == 0:
                            pe.wait_ge(t_lo, 4 * c + 4)
                        elif t >= 2:
                            pe.wait_ge(q_out, 4 * c + (t - 1))
                        triple(bank, [((wq_hi[:, k, rows], wq_lo[:, k, rows]), (aT_hi[:, k], aT_lo[:, k]))
                                      for k in range(KT)]).then_inc(q_ps, 1)
                    elif kind == "S":
                        if t == 0:
                            pe.wait_ge(q_lo, 4 * c + 4)
                            if batch is not None:
                                pe.wait_ge(blk_set, 4 * batch + 2)
                        elif isinstance(c, int) and c == 0:
                            wait(pe, s_sub, t - 1)
                        else:
                            pe.wait_ge(s_sub, 4 * c + t)
                        for g in range(KT):
                            into = halves(c, t)[:, g // 2, (g % 2) * GH * SC:(g % 2 + 1) * GH * SC]
                            kh, kl = (kblk[:, a, g].rearrange("p h k -> p (h k)") for a in range(2))
                            masked = batch is not None and t == 0
                            if masked:
                                nc.tensor.matmul(into, ident_bf[:, :], causal[:, :, :].rearrange("p h k -> p (h k)"),
                                                 start=True, stop=False)
                            for i, (s, m) in enumerate(((qT_hi, kh), (qT_hi, kl), (qT_lo, kh))):
                                last = nc.tensor.matmul(into, s[:, g, rows], m, start=(i == 0 and not masked),
                                                        stop=(i == 2))
                        last.then_inc(s_ps, 1)
                    elif kind == "Z":
                        pe.wait_ge(p_norm, 4 * c + t + 1)
                        first = isinstance(c, int) and c == 0
                        if first and t == 0:
                            pe.wait_ge(s_sub, TT)
                        for a in range(2):
                            if t == 2:
                                pe.wait_ge(v_lo, 4 * c + a + 1)
                            elif t % 2 and not first:
                                pe.wait_ge(z_lo, 8 * c + 2 * t + a - 1)
                            transposes(probs[t][:, a * D:(a + 1) * D], halves(c, t)[:, a], z_ps)
                    elif kind == "V":
                        pe.wait_ge(z_lo, 8 * c + 4 * (t // 2 + 1))
                        if batch is not None:
                            pe.wait_ge(blk_set, 4 * batch + 4)
                        for i in range(2):
                            m = 2 * (t % 2) + i
                            for n, (s, mv_) in enumerate(((0, pT_hi), (0, pT_lo), (1, pT_hi))):
                                for e in range(2):
                                    last = nc.tensor.matmul(
                                        at_ps[SC * e:SC * (e + 1), t % 2, i * HALF:(i + 1) * HALF],
                                        vblk[:, s, 2 * m + e], mv_[:, 2 * m + e], start=(n == 0), stop=(n == 2))
                        last.then_inc(v_ps, 1)
                    elif kind == "O":
                        if t == 0:
                            if isinstance(c, int) and c == 0:
                                pe.wait_ge(conv_lo, CONV_O)
                            pe.wait_ge(v_lo, 4 * c + 4)
                        elif t >= 2:
                            pe.wait_ge(x1_set, 4 * c + (t - 1))
                        triple(bank, [((aT_hi[:, k, rows], aT_lo[:, k, rows]), (wo_hi[:, k], wo_lo[:, k]))
                                      for k in range(KT)]).then_inc(o_ps, 1)
                    elif kind == "H":
                        pe.wait_ge(ln_out, 8 * c + (TT + t + 1))
                        if t < 2:
                            pe.wait_ge(x1_set, 4 * c + (t + 3))
                        else:
                            pe.wait_ge(h_lo, 4 * c + (t - 1))
                        transposes(xhat[:, t % 2, :], bank, h_ps)

                old = hT[1 - par]
                for g in range(GROUPS):
                    if isinstance(c, int) and c == 0 and 2 * g == BIAS_ROWS_AT:
                        for n in range(N1):
                            pe.wait_ge(w_loaded[W_1 + n], 16)
                        pe.wait_ge(kv_full_set, KT + 2)
                        bias_rows(1, B2LN, lambda k, m: w1_raw[m][:, k])
                    if isinstance(c, int) and c == 0 and 2 * g == BIAS_COLUMNS_AT:
                        bias_columns(1, D, bias_rows_sb)
                    if ff and g < NJ:
                        if g % KT == 0 and isinstance(c, int) and c == 1:
                            pe.wait_ge(conv_lo, conv_w1[g // KT])
                        if g == 0:
                            pe.wait_ge(h_lo, 4 * c)
                        if g >= 2:
                            pe.wait_ge(g_full, NJ * c + (g - 1 - NJ))
                        else:
                            wait(pe, g_full, NJ * c + (-NJ))
                        cut = slice(g % KT * P, (g % KT + 1) * P)
                        w1_hi, w1_lo = (w1_pairs[:, g // KT, a] for a in range(2))
                        triple(ff1_ps[:, g % 2, :], [((w1_hi[:, k, cut], w1_lo[:, k, cut]), (old[:, 0, k], old[:, 1, k]))
                                                     for k in range(KT)]).then_inc(ff1_done, 1)
                    if attn:
                        for kind, t in plan(c, 2 * g):
                            step(kind, t)
                    if ff and g >= LAG:
                        j = g - LAG
                        pe.wait_ge(g_lo, NJ * c + (j + 1 - NJ))
                        if j == 0:
                            wait(pe, out_set, 4 * c + (-TT))
                        if isinstance(c, int) and c == 1:
                            pe.wait_ge(conv_lo, conv_w2[j // KT] - KT + j % KT + 1)
                        pair = g_pair[j % NG]
                        for t in range(TT):
                            rows = slice(t * P, (t + 1) * P)
                            for i, (s, m) in enumerate(((0, w2_hi), (0, w2_lo), (1, w2_hi))):
                                last = nc.tensor.matmul(ff2_ps[:, t, :], pair[:, s, rows], m[:, j],
                                                        start=(j == 0 and i == 0), stop=(j == NJ - 1 and i == 2))
                            if j == NJ - 1:
                                last.then_inc(ff2_done, 1)
                    if attn:
                        for kind, t in plan(c, 2 * g + 1):
                            step(kind, t)

            slots(pe, slot)


INPUTS = ["x", "ctx_1024"] + ["L0_xattn_" + n for n in (
    "wq", "wk", "wv", "bq", "bk", "bv", "wo", "bo", "ln1_g", "ln1_b", "ln2_g", "ln2_b", "w1", "b1", "w2", "b2")]


def kernel(**inputs):
    import concourse.bacc as bacc
    from concourse.bass_utils import run_bass_kernel_spmd

    nc = bacc.Bacc("TRN2", target_bir_lowering=False, num_devices=1, dynamic_dma_scratch_size=1024)
    arrays, args = {}, []
    for name in INPUTS:
        a = np.ascontiguousarray(inputs[name])
        arrays[f"in_{name}"] = a
        args.append(nc.dram_tensor(f"in_{name}", a.shape, mybir.dt.from_np(a.dtype), kind="ExternalInput").ap())
    out = nc.dram_tensor("out_x", (BATCH, SQ, D), F32, kind="ExternalOutput").ap()
    cross_attention_block(nc, *args, out)
    r = run_bass_kernel_spmd(nc, [arrays], core_ids=[0])
    return r.results[0]["out_x"]
```
